# Optimizing a Trainium2 kernel written in Bass

```python
import numpy as np
import jax
import jax.numpy as jnp

def _softmax(x, axis=-1):
    return jax.nn.softmax(x, axis=axis)

def _gelu(x):
    return jax.nn.gelu(x, approximate=True)

def _silu(x):
    return jax.nn.silu(x)

def _sigmoid(x):
    return jax.nn.sigmoid(x)

def _layernorm(x, axis=-1, eps=1e-05):
    m = jnp.mean(x, axis=axis, keepdims=True)
    v = jnp.var(x, axis=axis, keepdims=True)
    return (x - m) / jnp.sqrt(v + eps)

def _scatter_add(tgt, idx, src, axis=0):
    return tgt.at[idx].add(src)

def _segment_sum(src, seg, n):
    return jax.ops.segment_sum(src, seg, n)
kernel_name = 'mk_dlrm_tower_d1_rec_r8_4b391d'

def setup_inputs(seed: int=0):
    np.random.seed(seed)
    _w = jnp.asarray

    def _rec_inputs():
        import jax
        import jax.numpy as jnp
        _tk = jax.random.key(seed)
        dense_ctx = jax.random.normal(jax.random.fold_in(_tk, 190), (512, 16), jnp.float32)
        ids = jnp.stack([jax.random.randint(jax.random.fold_in(_tk, 200 + f), (512,), 0, v, jnp.int32) for f, v in enumerate([125000, 125000, 1000, 125000, 1250, 1250, 12500, 12500, 1250, 1250, 1000, 1250, 12500, 12500, 12500, 1000, 1250, 12500, 1000, 1250, 1000, 1250, 12500, 1000, 1000, 1000, 1250, 1250, 1000, 1000, 1000, 1000, 1000, 1000, 1000, 1000, 1000, 1250, 1250])], axis=1)
        tbl_0 = 0.05 * jax.random.normal(jax.random.fold_in(_tk, 500 + 0), (125000, 64), jnp.float32)
        tbl_1 = 0.05 * jax.random.normal(jax.random.fold_in(_tk, 500 + 1), (125000, 64), jnp.float32)
        tbl_2 = 0.05 * jax.random.normal(jax.random.fold_in(_tk, 500 + 2), (1000, 64), jnp.float32)
        tbl_3 = 0.05 * jax.random.normal(jax.random.fold_in(_tk, 500 + 3), (125000, 64), jnp.float32)
        tbl_4 = 0.05 * jax.random.normal(jax.random.fold_in(_tk, 500 + 4), (1250, 64), jnp.float32)
        tbl_5 = 0.05 * jax.random.normal(jax.random.fold_in(_tk, 500 + 5), (1250, 64), jnp.float32)
        tbl_6 = 0.05 * jax.random.normal(jax.random.fold_in(_tk, 500 + 6), (12500, 64), jnp.float32)
        tbl_7 = 0.05 * jax.random.normal(jax.random.fold_in(_tk, 500 + 7), (12500, 64), jnp.float32)
        tbl_8 = 0.05 * jax.random.normal(jax.random.fold_in(_tk, 500 + 8), (1250, 64), jnp.float32)
        tbl_9 = 0.05 * jax.random.normal(jax.random.fold_in(_tk, 500 + 9), (1250, 64), jnp.float32)
        tbl_10 = 0.05 * jax.random.normal(jax.random.fold_in(_tk, 500 + 10), (1000, 64), jnp.float32)
        tbl_11 = 0.05 * jax.random.normal(jax.random.fold_in(_tk, 500 + 11), (1250, 64), jnp.float32)
        tbl_12 = 0.05 * jax.random.normal(jax.random.fold_in(_tk, 500 + 12), (12500, 64), jnp.float32)
        tbl_13 = 0.05 * jax.random.normal(jax.random.fold_in(_tk, 500 + 13), (12500, 64), jnp.float32)
        tbl_14 = 0.05 * jax.random.normal(jax.random.fold_in(_tk, 500 + 14), (12500, 64), jnp.float32)
        tbl_15 = 0.05 * jax.random.normal(jax.random.fold_in(_tk, 500 + 15), (1000, 64), jnp.float32)
        tbl_16 = 0.05 * jax.random.normal(jax.random.fold_in(_tk, 500 + 16), (1250, 64), jnp.float32)
        tbl_17 = 0.05 * jax.random.normal(jax.random.fold_in(_tk, 500 + 17), (12500, 64), jnp.float32)
        tbl_18 = 0.05 * jax.random.normal(jax.random.fold_in(_tk, 500 + 18), (1000, 64), jnp.float32)
        tbl_19 = 0.05 * jax.random.normal(jax.random.fold_in(_tk, 500 + 19), (1250, 64), jnp.float32)
        tbl_20 = 0.05 * jax.random.normal(jax.random.fold_in(_tk, 500 + 20), (1000, 64), jnp.float32)
        tbl_21 = 0.05 * jax.random.normal(jax.random.fold_in(_tk, 500 + 21), (1250, 64), jnp.float32)
        tbl_22 = 0.05 * jax.random.normal(jax.random.fold_in(_tk, 500 + 22), (12500, 64), jnp.float32)
        tbl_23 = 0.05 * jax.random.normal(jax.random.fold_in(_tk, 500 + 23), (1000, 64), jnp.float32)
        tbl_24 = 0.05 * jax.random.normal(jax.random.fold_in(_tk, 500 + 24), (1000, 64), jnp.float32)
        tbl_25 = 0.05 * jax.random.normal(jax.random.fold_in(_tk, 500 + 25), (1000, 64), jnp.float32)
        tbl_26 = 0.05 * jax.random.normal(jax.random.fold_in(_tk, 500 + 26), (1250, 64), jnp.float32)
        tbl_27 = 0.05 * jax.random.normal(jax.random.fold_in(_tk, 500 + 27), (1250, 64), jnp.float32)
        tbl_28 = 0.05 * jax.random.normal(jax.random.fold_in(_tk, 500 + 28), (1000, 64), jnp.float32)
        tbl_29 = 0.05 * jax.random.normal(jax.random.fold_in(_tk, 500 + 29), (1000, 64), jnp.float32)
        tbl_30 = 0.05 * jax.random.normal(jax.random.fold_in(_tk, 500 + 30), (1000, 64), jnp.float32)
        tbl_31 = 0.05 * jax.random.normal(jax.random.fold_in(_tk, 500 + 31), (1000, 64), jnp.float32)
        tbl_32 = 0.05 * jax.random.normal(jax.random.fold_in(_tk, 500 + 32), (1000, 64), jnp.float32)
        tbl_33 = 0.05 * jax.random.normal(jax.random.fold_in(_tk, 500 + 33), (1000, 64), jnp.float32)
        tbl_34 = 0.05 * jax.random.normal(jax.random.fold_in(_tk, 500 + 34), (1000, 64), jnp.float32)
        tbl_35 = 0.05 * jax.random.normal(jax.random.fold_in(_tk, 500 + 35), (1000, 64), jnp.float32)
        tbl_36 = 0.05 * jax.random.normal(jax.random.fold_in(_tk, 500 + 36), (1000, 64), jnp.float32)
        tbl_37 = 0.05 * jax.random.normal(jax.random.fold_in(_tk, 500 + 37), (1250, 64), jnp.float32)
        tbl_38 = 0.05 * jax.random.normal(jax.random.fold_in(_tk, 500 + 38), (1250, 64), jnp.float32)
        _rk = jax.random.fold_in(_tk, 7)
        W_top1 = 0.0363456 * jax.random.normal(jax.random.fold_in(_tk, 801), (757, 512), jnp.float32)
        W_top2 = 0.0441942 * jax.random.normal(jax.random.fold_in(_tk, 802), (512, 256), jnp.float32)
        W_top3 = 0.0625 * jax.random.normal(jax.random.fold_in(_tk, 803), (256, 1), jnp.float32)
        b_top1 = jnp.zeros((512,), jnp.float32)
        b_top2 = jnp.zeros((256,), jnp.float32)
        return (dense_ctx, ids, tbl_0, tbl_1, tbl_2, tbl_3, tbl_4, tbl_5, tbl_6, tbl_7, tbl_8, tbl_9, tbl_10, tbl_11, tbl_12, tbl_13, tbl_14, tbl_15, tbl_16, tbl_17, tbl_18, tbl_19, tbl_20, tbl_21, tbl_22, tbl_23, tbl_24, tbl_25, tbl_26, tbl_27, tbl_28, tbl_29, tbl_30, tbl_31, tbl_32, tbl_33, tbl_34, tbl_35, tbl_36, tbl_37, tbl_38, W_top1, b_top1, W_top2, b_top2, W_top3)
    dense_ctx, ids, tbl_0, tbl_1, tbl_2, tbl_3, tbl_4, tbl_5, tbl_6, tbl_7, tbl_8, tbl_9, tbl_10, tbl_11, tbl_12, tbl_13, tbl_14, tbl_15, tbl_16, tbl_17, tbl_18, tbl_19, tbl_20, tbl_21, tbl_22, tbl_23, tbl_24, tbl_25, tbl_26, tbl_27, tbl_28, tbl_29, tbl_30, tbl_31, tbl_32, tbl_33, tbl_34, tbl_35, tbl_36, tbl_37, tbl_38, W_top1, b_top1, W_top2, b_top2, W_top3 = _rec_inputs()

    def _L0_rec_setup():
        import jax, jax.numpy as jnp
        import numpy as np
        NUM_FIELDS = 39
        _ROW, _COL = np.triu_indices(NUM_FIELDS, k=1)
        key = jax.random.key(seed)
        x = jax.random.normal(key, (2048, NUM_FIELDS, 64), dtype=jnp.float32)
        return {'x': x}
    _L0_rec_all = _L0_rec_setup()
    _L0_rec_in = {k: v for k, v in _L0_rec_all.items() if k in ()}
    del _L0_rec_all
    return {'dense_ctx': dense_ctx, 'ids': ids, 'tbl_0': tbl_0, 'tbl_1': tbl_1, 'tbl_2': tbl_2, 'tbl_3': tbl_3, 'tbl_4': tbl_4, 'tbl_5': tbl_5, 'tbl_6': tbl_6, 'tbl_7': tbl_7, 'tbl_8': tbl_8, 'tbl_9': tbl_9, 'tbl_10': tbl_10, 'tbl_11': tbl_11, 'tbl_12': tbl_12, 'tbl_13': tbl_13, 'tbl_14': tbl_14, 'tbl_15': tbl_15, 'tbl_16': tbl_16, 'tbl_17': tbl_17, 'tbl_18': tbl_18, 'tbl_19': tbl_19, 'tbl_20': tbl_20, 'tbl_21': tbl_21, 'tbl_22': tbl_22, 'tbl_23': tbl_23, 'tbl_24': tbl_24, 'tbl_25': tbl_25, 'tbl_26': tbl_26, 'tbl_27': tbl_27, 'tbl_28': tbl_28, 'tbl_29': tbl_29, 'tbl_30': tbl_30, 'tbl_31': tbl_31, 'tbl_32': tbl_32, 'tbl_33': tbl_33, 'tbl_34': tbl_34, 'tbl_35': tbl_35, 'tbl_36': tbl_36, 'tbl_37': tbl_37, 'tbl_38': tbl_38, 'W_top1': W_top1, 'b_top1': b_top1, 'W_top2': W_top2, 'b_top2': b_top2, 'W_top3': W_top3}

def reference(dense_ctx, ids, tbl_0, tbl_1, tbl_2, tbl_3, tbl_4, tbl_5, tbl_6, tbl_7, tbl_8, tbl_9, tbl_10, tbl_11, tbl_12, tbl_13, tbl_14, tbl_15, tbl_16, tbl_17, tbl_18, tbl_19, tbl_20, tbl_21, tbl_22, tbl_23, tbl_24, tbl_25, tbl_26, tbl_27, tbl_28, tbl_29, tbl_30, tbl_31, tbl_32, tbl_33, tbl_34, tbl_35, tbl_36, tbl_37, tbl_38, W_top1, b_top1, W_top2, b_top2, W_top3):
    import jax
    import jax.numpy as jnp

    def _L0_rec_ref(x):
        import jax, jax.numpy as jnp
        import numpy as np
        NUM_FIELDS = 39
        _ROW, _COL = np.triu_indices(NUM_FIELDS, k=1)
        s = jnp.sum(x, axis=-1)
        return s[:, _ROW] * s[:, _COL]
    e = jnp.stack([tbl_0[ids[:, 0]], tbl_1[ids[:, 1]], tbl_2[ids[:, 2]], tbl_3[ids[:, 3]], tbl_4[ids[:, 4]], tbl_5[ids[:, 5]], tbl_6[ids[:, 6]], tbl_7[ids[:, 7]], tbl_8[ids[:, 8]], tbl_9[ids[:, 9]], tbl_10[ids[:, 10]], tbl_11[ids[:, 11]], tbl_12[ids[:, 12]], tbl_13[ids[:, 13]], tbl_14[ids[:, 14]], tbl_15[ids[:, 15]], tbl_16[ids[:, 16]], tbl_17[ids[:, 17]], tbl_18[ids[:, 18]], tbl_19[ids[:, 19]], tbl_20[ids[:, 20]], tbl_21[ids[:, 21]], tbl_22[ids[:, 22]], tbl_23[ids[:, 23]], tbl_24[ids[:, 24]], tbl_25[ids[:, 25]], tbl_26[ids[:, 26]], tbl_27[ids[:, 27]], tbl_28[ids[:, 28]], tbl_29[ids[:, 29]], tbl_30[ids[:, 30]], tbl_31[ids[:, 31]], tbl_32[ids[:, 32]], tbl_33[ids[:, 33]], tbl_34[ids[:, 34]], tbl_35[ids[:, 35]], tbl_36[ids[:, 36]], tbl_37[ids[:, 37]], tbl_38[ids[:, 38]]], axis=1)
    z = _L0_rec_ref(e)
    z = z.reshape(z.shape[0], -1)
    h = jnp.concatenate([z, dense_ctx], axis=1)
    h = jnp.maximum(h @ W_top1 + b_top1, 0.0)
    h = jnp.maximum(h @ W_top2 + b_top2, 0.0)
    y = h @ W_top3
    return y

_drawn_inputs = setup_inputs


def setup_inputs(seed=0):
    import zlib

    import numpy as np

    out = dict(_drawn_inputs(seed))
    spreads = {'b_top1': (0.0, 0.1), 'b_top2': (0.0, 0.1)}
    factors = {}
    for name, (base, spread) in spreads.items():
        noise = np.random.default_rng([zlib.crc32(name.encode()), seed]).standard_normal(out[name].shape)
        drawn = base * np.exp(spread * noise) if base else spread * noise
        out[name] = jnp.asarray(drawn.astype(out[name].dtype))
    for name, factor in factors.items():
        out[name] = (out[name] * factor).astype(out[name].dtype)
    return out
```

```python
import concourse.bass as bass
from concourse import mybir
from contextlib import ExitStack

P = 128
EMB = 64
BATCH = 512
NC = BATCH // P
ROWS = [125000, 125000, 1000, 125000, 1250, 1250, 12500, 12500, 1250, 1250, 1000, 1250, 12500, 12500, 12500,
        1000, 1250, 12500, 1000, 1250, 1000, 1250, 12500, 1000, 1000, 1000, 1250, 1250, 1000, 1000, 1000,
        1000, 1000, 1000, 1000, 1000, 1000, 1250, 1250]
NF = len(ROWS)
SMALL_ROWS = 1250
SMALL = sorted((f for f in range(NF) if ROWS[f] <= SMALL_ROWS), key=lambda f: -ROWS[f])
BIG = [f for f in range(NF) if ROWS[f] > SMALL_ROWS]
NS, NB = len(SMALL), len(BIG)
BLOCKS = [-(-ROWS[f] // P) for f in SMALL]
BLOCK_AT = [sum(BLOCKS[:t]) for t in range(NS + 1)]
GROUPS = [(0, 4), (4, 8), (8, 12), (12, 16), (16, 20), (20, 24), (24, 29)]
NG = len(GROUPS)
LATE = 3
EARLY = NB - LATE
assert EARLY == NG and all(len({BLOCKS[t] for t in range(*g)}) == 1 for g in GROUPS)
ORDER = [f for g, (a, b) in enumerate(GROUPS) for f in SMALL[a:b] + [BIG[g]]] + BIG[EARLY:]
GROUP_AT = [a + g for g, (a, b) in enumerate(GROUPS)]
BIG_AT = [b + g for g, (a, b) in enumerate(GROUPS)]
NEARLY = NF - LATE
EARLY_PAIRS = [(i, j) for j in range(NEARLY) for i in range(j)]
LATE_PAIRS = [(i, j) for j in range(NEARLY, NF) for i in range(j)]
KE = -(-len(EARLY_PAIRS) // P)
KC = KE + 1
NL = len(LATE_PAIRS)
DENSE = 16
assert NL + DENSE + 1 == P
NEEDS = [max(j for _, j in EARLY_PAIRS[k * P:(k + 1) * P]) + 1 for k in range(KE)]
STAGES = [GROUP_AT[4] - 1, GROUP_AT[5] - 1, GROUP_AT[6] - 1, NEARLY]
STAGE_OF = [next(s for s, n in enumerate(STAGES) if n >= need) for need in NEEDS]
assert STAGE_OF == [0, 1, 2, 3, 3]
H1, H2 = 512, 256
N1, N2 = H1 // P, H2 // P
KINDS = 5
QF = 32
HOT = 4


def build_tower(nc, ids_rows, ids_cols, tables, big, kind_coef, pick, ident, dense_t, w1, w2, b2, w3, out):
    fp32, bf16, i32 = mybir.dt.float32, mybir.dt.bfloat16, mybir.dt.int32
    ALU = mybir.AluOpType
    ACT = mybir.ActivationFunctionType
    AX = mybir.AxisListType

    with ExitStack() as ctx:
        def sb(name, shape, dt):
            return ctx.enter_context(nc.sbuf_tensor(name, shape, dt))

        def ps(name, shape, dt):
            return ctx.enter_context(nc.psum_tensor(name, shape, dt))

        def sem(name):
            return ctx.enter_context(nc.semaphore(name))

        idr = sb("idr", [P, NC * NF], i32)
        idc = sb("idc", [P, P], i32)
        tab = sb("tab", [P, BLOCK_AT[NS], EMB], fp32)
        cut = sb("cut", [P, 3 * BLOCK_AT[NS]], fp32)
        qi = sb("qi", [P, P], i32)
        q2 = sb("q2", [P, P], i32)
        q2h = sb("q2h", [P, P], i32)
        q2l = sb("q2l", [P, P], i32)
        kinds = sb("kinds", [P, KINDS, P], bf16)
        hot_rows = sb("hot_rows", [KINDS, QF * BATCH], bf16)
        coef = sb("coef", [KINDS, P], bf16)
        hot = sb("hot", [P, NS, BATCH], bf16)
        blk = sb("blk", [P, NC, NS], i32)
        count = sb("count", [P, max(BLOCKS)], i32)
        mask = sb("mask", [P, NC * BLOCK_AT[NS]], bf16)
        prod = sb("prod", [P, 2, 512], fp32)
        row_e = sb("row_e", [P, EARLY, NC, EMB], fp32)
        row_l = sb("row_l", [P, NC, LATE, EMB], fp32)
        sums = sb("sums", [P, NC, 3, NF], fp32)
        sums_t = sb("sums_t", [3 * NF, NC, P], bf16)
        picks = sb("picks", [3 * NF, 2, KE * P + NL], bf16)
        idn = sb("idn", [P, P], bf16)
        first = sb("first", [P, 2, BATCH], fp32)
        z = sb("z", [P, KC, BATCH], fp32)
        w1s = sb("w1s", [P, KC, H1], fp32)
        w2s = sb("w2s", [P, N1, H2], fp32)
        w3s = sb("w3s", [P, N2], fp32)
        b2s = sb("b2s", [P, N2], fp32)
        h1 = sb("h1", [P, N1, BATCH], fp32)
        h2 = sb("h2", [P, N2, BATCH], fp32)
        y = sb("y", [1, BATCH], fp32)

        acc = ps("acc", [P, N1, BATCH], fp32)
        pk0 = ps("pk0", [P, 512], fp32)
        pk1 = ps("pk1", [P, 512], fp32)
        fa = ps("fa", [P, 512], fp32)
        fb = ps("fb", [P, 512], fp32)
        pk = [pk0, pk1]

        ids_rows_in, ids_cols_in, coef_in = sem("ids_rows_in"), sem("ids_cols_in"), sem("coef_in")
        table_in = [sem(f"table_in{n}") for n in range(2 * NG)]
        early_in = [sem(f"early_in{n}") for n in range(EARLY)]
        late_in = [sem(f"late_in{c}") for c in range(NC)]
        picks_in, ident_in, dense_in = sem("picks_in"), sem("ident_in"), sem("dense_in")
        w1_in, w2_in, tail_in = sem("w1_in"), sem("w2_in"), sem("tail_in")
        cleared = sem("cleared")
        kinds_ready = sem("kinds_ready")
        hot_rows_in = sem("hot_rows_in")
        arg_ready = sem("arg_ready")
        hot_ready = sem("hot_ready")
        cut_ready = sem("cut_ready")
        picked = sem("picked")
        masked = sem("masked")
        sums_ready = sem("sums_ready")
        turned = sem("turned")
        sums_t_ready = sem("sums_t_ready")
        factors = sem("factors")
        first_ready = sem("first_ready")
        z_ready = sem("z_ready")
        layer1 = sem("layer1")
        h1_ready = sem("h1_ready")
        layer2 = sem("layer2")
        h2_ready = sem("h2_ready")
        layer3 = sem("layer3")
        y_ready = sem("y_ready")
        y_out = sem("y_out")
        dve_step = sem("dve_step")

        def upper(ap):
            names = " ".join("abcd"[:len(ap.shape) - 1])
            halves_of = ap.bitcast(bf16).rearrange(f"{names} (y u) -> {names} y u", u=2)
            return halves_of[(slice(None),) * len(ap.shape) + (1,)]

        def cut_of(a, b, part):
            n = BLOCKS[a]
            return cut[:, 3 * BLOCK_AT[a]:3 * BLOCK_AT[b]].rearrange(
                "p (t k j) -> p t k j", k=3, j=n)[:, :, part, :]

        def mask_of(g):
            a, b = GROUPS[g]
            return mask[:, NC * BLOCK_AT[a]:NC * BLOCK_AT[b]]

        halves = [((a, a + 2), (a + 2, b)) for a, b in GROUPS]
        block = ctx.enter_context(nc.Block())

        @block.sync
        def _(sp):
            sp.dma_start(idr[:, :], ids_rows).then_inc(ids_rows_in, 16)
            sp.dma_start(coef[:, :], kind_coef).then_inc(coef_in, 16)
            for g in range(NG):
                for n, (a, b) in enumerate(halves[g]):
                    sp.dma_start(tab[:, BLOCK_AT[a]:BLOCK_AT[b], :],
                                 tables[:, BLOCK_AT[a]:BLOCK_AT[b], :]).then_inc(table_in[2 * g + n], 16)
                if g == 3:
                    sp.dma_start(picks[:, :, :], pick).then_inc(picks_in, 16)
                    sp.dma_start(idn[:, :], ident).then_inc(ident_in, 16)
                    sp.dma_start(w1s[:, :, :], w1).then_inc(w1_in, 16)
            sp.dma_start(z[NL:P, KE, :], dense_t).then_inc(dense_in, 16)
            sp.dma_start(w2s[:, :, :], w2).then_inc(w2_in, 16)
            sp.dma_start(w3s[:, :], w3).then_inc(tail_in, 16)
            sp.dma_start(b2s[:, :], b2).then_inc(tail_in, 16)
            sp.wait_ge(y_ready, NC)
            sp.dma_start(out, y[:, :]).then_inc(y_out, 16)
            sp.wait_ge(y_out, 16)

        @block.gpsimd
        def _(pool):
            nc.gpsimd.iota(count[:, :], pattern=[[1, max(BLOCKS)]], base=0, channel_multiplier=0).then_inc(cleared, 1)
            nc.gpsimd.memset(sums[:, :, :, :], 0.0).then_inc(cleared, 1)
            pool.wait_ge(ids_rows_in, 16)

            def gather(rows, n, c, done):
                at = c * NF + NS + n
                pool.indirect_dma_start(
                    out=rows, out_offset=None, in_=big[n][:, :],
                    in_offset=bass.IndirectOffsetOnAxis(ap=idr[:, at:at + 1], axis=0)).then_inc(done, 16)

            for n in range(EARLY):
                for c in range(NC):
                    gather(row_e[:, n, c, :], n, c, early_in[n])
            for c in range(NC):
                for n in range(LATE):
                    gather(row_l[:, c, n, :], EARLY + n, c, late_in[c])

        @block.scalar
        def _(act):
            act.dma_start(idc[:, :], ids_cols).then_inc(ids_cols_in, 16)
            act.wait_ge(kinds_ready, KINDS)
            for k in range(KINDS):
                act.dma_start(hot_rows[k:k + 1, :], kinds[:, k, :]).then_inc(hot_rows_in, 16)
            for t in range(NS):
                act.wait_ge(arg_ready, t + 1)
                nc.scalar.activation(hot[:, t, :], acc[:, t % HOT, :], ACT.Relu).then_inc(hot_ready, 1)

            def sums_t_copy(n, lo, hi):
                act.wait_ge(turned, n + 1)
                nc.scalar.activation(sums_t[:, lo:hi, :],
                                     fa[0:3 * NF, 0:(hi - lo) * P // 2].bitcast(bf16).rearrange(
                                         "p (c x) -> p c x", x=P), ACT.Copy).then_inc(sums_t_ready, 1)

            def first_copy(n, rows, width):
                act.wait_ge(factors, n + 1)
                if n >= 2:
                    act.wait_ge(z_ready, n - 1)
                nc.scalar.activation(first[0:rows, n % 2, 0:width], fa[0:rows, 0:width],
                                     ACT.Copy).then_inc(first_ready, 1)

            for s in range(len(STAGES)):
                sums_t_copy(s, 0, NC)
                for k in range(KE):
                    if STAGE_OF[k] == s:
                        first_copy(k, P, BATCH)
            act.wait_ge(tail_in, 32)
            for c in range(NC + 1):
                if c < NC:
                    sums_t_copy(len(STAGES) + c, c, c + 1)
                    first_copy(KE + c, NL, P)
                if c < NC:
                    act.wait_ge(layer1, c + 1)
                    nc.scalar.activation(h1[:, :, c * P:(c + 1) * P], acc[:, :, c * P:(c + 1) * P],
                                         ACT.Relu).then_inc(h1_ready, 1)
                if c >= 1:
                    e = c - 1
                    act.wait_ge(layer2, 2 * e + 2)
                    nc.scalar.activation(h2[:, 1, e * P:(e + 1) * P], pk1[:, 0:P], ACT.Relu,
                                         bias=b2s[:, 1:2]).then_inc(h2_ready, 1)

        @block.vector
        def _(dve):
            steps = [0]

            def then_wait(ins):
                steps[0] += 1
                ins.then_inc(dve_step, 1)
                dve.wait_ge(dve_step, steps[0])

            nc.vector.memset(kinds[:, 3:KINDS, :], 1.0).then_inc(kinds_ready, 2)
            dve.wait_ge(ids_cols_in, 16)
            then_wait(nc.vector.tensor_single_scalar(qi[:, :], idc[:, :], P - 1, ALU.bitwise_and))
            nc.vector.tensor_copy(kinds[:, 0, :], qi[:, :]).then_inc(kinds_ready, 1)
            then_wait(nc.vector.tensor_tensor(q2[:, :], qi[:, :], qi[:, :], ALU.mult))
            nc.vector.tensor_single_scalar(q2h[:, :], q2[:, :], P * P - P, ALU.bitwise_and)
            then_wait(nc.vector.tensor_single_scalar(q2l[:, :], q2[:, :], P - 1, ALU.bitwise_and))
            nc.vector.tensor_copy(kinds[:, 1, :], q2h[:, :]).then_inc(kinds_ready, 1)
            nc.vector.tensor_copy(kinds[:, 2, :], q2l[:, :]).then_inc(kinds_ready, 1)
            dve.wait_ge(ids_rows_in, 16)
            dve.wait_ge(cleared, 2)
            then_wait(nc.vector.tensor_single_scalar(
                blk[:, :, :], idr[:, :].rearrange("p (c f) -> p c f", c=NC)[:, :, 0:NS], 7, ALU.arith_shift_right))
            for g, (a, b) in enumerate(GROUPS):
                n = BLOCKS[a]
                last = nc.vector.tensor_tensor(
                    mask_of(g).rearrange("p (c t j) -> p c t j", c=NC, j=n),
                    blk[:, :, a:b].unsqueeze(3).to_broadcast([P, NC, b - a, n]),
                    count[:, 0:n].unsqueeze(1).unsqueeze(1).to_broadcast([P, NC, b - a, n]), ALU.is_equal)
            then_wait(last)

            def row_sums(g, n):
                a, b = halves[g][n]
                dve.wait_ge(table_in[2 * g + n], 16)
                last = nc.vector.tensor_reduce(
                    cut_of(a, b, 0), tab[:, BLOCK_AT[a]:BLOCK_AT[b], :].rearrange("p (t j) x -> p t j x", j=BLOCKS[a]),
                    axis=AX.X, op=ALU.add)
                if n == 1:
                    then_wait(last)
                return last

            def cut_sums(g):
                a, b = GROUPS[g]
                then_wait(nc.vector.tensor_tensor(cut_of(a, b, 1), cut_of(a, b, 0), upper(cut_of(a, b, 0)),
                                                  ALU.subtract))
                nc.vector.tensor_tensor(cut_of(a, b, 2), cut_of(a, b, 1), upper(cut_of(a, b, 1)),
                                        ALU.subtract).then_inc(cut_ready, 1)

            def pick_blocks(g):
                a, b = GROUPS[g]
                n, w = BLOCKS[a], NC * 3 * (BLOCK_AT[b] - BLOCK_AT[a])
                dve.wait_ge(picked, g + 1)
                nc.vector.tensor_tensor(
                    prod[:, g % 2, 0:w].rearrange("p (m k j) -> p m k j", k=3, j=n),
                    pk[g % 2][:, 0:w].rearrange("p (m k j) -> p m k j", k=3, j=n),
                    mask_of(g).rearrange("p (m j) -> p m j", j=n).unsqueeze(2).to_broadcast([P, NC * (b - a), 3, n]),
                    ALU.mult).then_inc(masked, 1)
                dve.wait_ge(masked, g + 1)
                then_wait(nc.vector.tensor_reduce(
                    sums[:, :, 0, GROUP_AT[g]:GROUP_AT[g] + b - a],
                    prod[:, g % 2, 0:w].rearrange("p (c t x) -> p c t x", c=NC, x=3 * n), axis=AX.X, op=ALU.add))

            def big_sums(n):
                dve.wait_ge(early_in[n], 16 * NC)
                then_wait(nc.vector.tensor_reduce(sums[:, :, 0, BIG_AT[n]:BIG_AT[n] + 1], row_e[:, n, :, :],
                                                  axis=AX.X, op=ALU.add))

            def cut_stage(s):
                lo, hi = ([0] + STAGES)[s], STAGES[s]
                then_wait(nc.vector.tensor_tensor(sums[:, :, 1, lo:hi], sums[:, :, 0, lo:hi],
                                                  upper(sums[:, :, 0, lo:hi]), ALU.subtract))
                nc.vector.tensor_tensor(sums[:, :, 2, lo:hi], sums[:, :, 1, lo:hi],
                                        upper(sums[:, :, 1, lo:hi]), ALU.subtract).then_inc(sums_ready, 1)

            def products(k):
                dve.wait_ge(first_ready, k + 1)
                nc.vector.tensor_tensor(z[:, k, :], first[:, k % 2, :], fb[:, :], ALU.mult).then_inc(z_ready, 1)

            row_sums(0, 0)
            row_sums(0, 1)
            cut_sums(0)
            for g in range(1, NG):
                row_sums(g, 0)
                pick_blocks(g - 1)
                if g <= 3:
                    big_sums(g - 1)
                if g == 5:
                    big_sums(3)
                if g == 6:
                    big_sums(4)
                if g >= 4:
                    cut_stage(g - 4)
                row_sums(g, 1)
                cut_sums(g)
                if g >= 4:
                    products(g - 4)
            big_sums(5)
            big_sums(6)
            pick_blocks(6)
            cut_stage(3)
            products(3)
            products(4)
            dve.wait_ge(tail_in, 32)
            for c in range(NC + 1):
                if c < NC:
                    dve.wait_ge(late_in[c], 16 * LATE)
                    then_wait(nc.vector.tensor_reduce(sums[:, c, 0, NEARLY:NF], row_l[:, c, :, :],
                                                      axis=AX.X, op=ALU.add))
                    then_wait(nc.vector.tensor_tensor(sums[:, c, 1, NEARLY:NF], sums[:, c, 0, NEARLY:NF],
                                                      upper(sums[:, c, 0, NEARLY:NF]), ALU.subtract))
                    nc.vector.tensor_tensor(sums[:, c, 2, NEARLY:NF], sums[:, c, 1, NEARLY:NF],
                                            upper(sums[:, c, 1, NEARLY:NF]), ALU.subtract).then_inc(sums_ready, 1)
                    dve.wait_ge(first_ready, KE + c + 1)
                    nc.vector.tensor_tensor(z[0:NL, KE, c * P:(c + 1) * P], first[0:NL, (KE + c) % 2, 0:P],
                                            fb[0:NL, 0:P], ALU.mult).then_inc(z_ready, 1)
                if c >= 1:
                    e = c - 1
                    dve.wait_ge(layer2, 2 * e + 1)
                    nc.vector.tensor_scalar(h2[:, 0, e * P:(e + 1) * P], pk0[:, 0:P], b2s[:, 0:1], 0.0,
                                            ALU.add, ALU.max).then_inc(h2_ready, 1)
                    dve.wait_ge(layer3, e + 1)
                    nc.vector.tensor_copy(y[:, e * P:(e + 1) * P], fb[0:1, P:2 * P]).then_inc(y_ready, 1)

        @block.tensor
        def _(pe):
            def hot_arg(t):
                if t >= HOT:
                    pe.wait_ge(hot_ready, t - HOT + 1)
                nc.tensor.matmul(acc[:, t % HOT, :], coef[:, :], hot_rows[:, t * BATCH:(t + 1) * BATCH],
                                 start=True, stop=True).then_inc(arg_ready, 1)

            def pick_rows(g):
                a, b = GROUPS[g]
                n, w = 3 * BLOCKS[a], b - a
                pe.wait_ge(cut_ready, g + 1)
                pe.wait_ge(hot_ready, b)
                if g >= 2:
                    pe.wait_ge(masked, g - 1)
                for c in range(NC):
                    for t in range(a, b):
                        at = (c * w + t - a) * n
                        last = nc.tensor.matmul(pk[g % 2][:, at:at + n], hot[:, t, c * P:(c + 1) * P],
                                                upper(cut[:, 3 * BLOCK_AT[t]:3 * BLOCK_AT[t + 1]]),
                                                start=True, stop=True)
                last.then_inc(picked, 1)

            def turn(n, lo, hi):
                pe.wait_ge(sums_ready, n + 1)
                for c in range(lo, hi):
                    last = nc.tensor.transpose(fa[0:3 * NF, (c - lo) * P // 2:(c - lo + 1) * P // 2].bitcast(bf16),
                                               upper(sums[:, c, :, :].rearrange("p k f -> p (k f)")), idn[:, :])
                last.then_inc(turned, 1)

            def both_factors(n, k, lo, hi, rows):
                if k < KE and STAGE_OF[k] == (STAGE_OF[k - 1] if k else -1):
                    pe.wait_ge(z_ready, n)
                for side, bank in ((0, fa), (1, fb)):
                    last = nc.tensor.matmul(bank[0:rows, 0:(hi - lo) * P], picks[:, side, k * P:k * P + rows],
                                            sums_t[:, lo:hi, :], start=True, stop=True)
                last.then_inc(factors, 1)

            def layer1_part(k, lo, hi):
                for n in range(N1):
                    last = nc.tensor.matmul(acc[:, n, lo * P:hi * P], w1s[:, k, n * P:(n + 1) * P],
                                            z[:, k, lo * P:hi * P], start=(k == 0), stop=(k == KE),
                                            skip_group_check=True)
                return last

            pe.wait_ge(coef_in, 16)
            pe.wait_ge(hot_rows_in, 16 * KINDS)
            ahead = [9, 16, 23, NS] + [NS] * (NG - 4)
            done = 0
            for g in range(NG):
                for t in range(done, ahead[g]):
                    hot_arg(t)
                done = ahead[g]
                if g == 4:
                    pe.wait_ge(ident_in, 16)
                    pe.wait_ge(picks_in, 16)
                if g >= 4:
                    s = g - 4
                    if s >= 1:
                        pe.wait_ge(z_ready, s)
                    turn(s, 0, NC)
                    pe.wait_ge(sums_t_ready, s + 1)
                    both_factors(s, s, 0, NC, P)
                pick_rows(g)
                if g >= 4:
                    if s == 0:
                        pe.wait_ge(w1_in, 16)
                        pe.wait_ge(hot_ready, NS)
                    pe.wait_ge(z_ready, s + 1)
                    layer1_part(s, 0, NC)
            turn(3, 0, NC)
            pe.wait_ge(sums_t_ready, 4)
            both_factors(3, 3, 0, NC, P)
            both_factors(4, 4, 0, NC, P)
            layer1_part(3, 0, NC)
            pe.wait_ge(z_ready, 5)
            layer1_part(4, 0, NC)
            pe.wait_ge(dense_in, 16)
            pe.wait_ge(w2_in, 16)
            for c in range(NC + 1):
                if c < NC:
                    turn(4 + c, c, c + 1)
                    pe.wait_ge(sums_t_ready, 4 + c + 1)
                    both_factors(KE + c, KE, c, c + 1, NL)
                    pe.wait_ge(z_ready, KE + c + 1)
                    layer1_part(KE, c, c + 1).then_inc(layer1, 1)
                if c >= 1:
                    e = c - 1
                    pe.wait_ge(h1_ready, e + 1)
                    if e >= 1:
                        pe.wait_ge(h2_ready, 2 * e)
                    for m in range(N2):
                        for n in range(N1):
                            last = nc.tensor.matmul(pk[m][:, 0:P], w2s[:, n, m * P:(m + 1) * P],
                                                    h1[:, n, e * P:(e + 1) * P], start=(n == 0), stop=(n == N1 - 1))
                        last.then_inc(layer2, 1)
                    pe.wait_ge(h2_ready, 2 * e + 2)
                    if c < NC:
                        pe.wait_ge(z_ready, KE + c + 1)
                    for m in range(N2):
                        last = nc.tensor.matmul(fb[0:1, P:2 * P], w3s[:, m:m + 1], h2[:, m, e * P:(e + 1) * P],
                                                start=(m == 0), stop=(m == N2 - 1))
                    last.then_inc(layer3, 1)


def kernel(**inputs):
    import ml_dtypes
    import numpy as np
    import concourse.bacc as bacc
    from concourse.bass_utils import run_bass_kernel_spmd

    a = {k: np.asarray(v) for k, v in inputs.items()}
    ids = a["ids"]
    arrays = {}
    arrays["ids_rows"] = np.ascontiguousarray(
        ids[:, SMALL + BIG].reshape(NC, P, NF).transpose(1, 0, 2).reshape(P, NC * NF))
    cols = np.zeros((QF, BATCH), ids.dtype)
    cols[:NS] = ids[:, SMALL].T
    arrays["ids_cols"] = cols.reshape(P, P)
    tables = np.zeros((P, BLOCK_AT[NS], EMB), np.float32)
    for t, f in enumerate(SMALL):
        padded = np.zeros((BLOCKS[t] * P, EMB), np.float32)
        padded[:ROWS[f]] = a[f"tbl_{f}"]
        tables[:, BLOCK_AT[t]:BLOCK_AT[t + 1]] = padded.reshape(BLOCKS[t], P, EMB).transpose(1, 0, 2)
    arrays["tables"] = tables
    for n, f in enumerate(BIG):
        arrays[f"big{n}"] = np.ascontiguousarray(a[f"tbl_{f}"])
    p = np.arange(P)
    rest = 1 - p * p
    arrays["kind_coef"] = np.stack([2 * p, 0 * p - 1, 0 * p - 1, rest // P * P, rest % P]).astype(ml_dtypes.bfloat16)
    pick = np.zeros((3, NF, 2, KE * P + NL), ml_dtypes.bfloat16)
    for at, pairs in ((0, EARLY_PAIRS), (KE * P, LATE_PAIRS)):
        for n, (i, j) in enumerate(pairs):
            pick[:, i, 0, at + n] = 1
            pick[:, j, 1, at + n] = 1
    arrays["pick"] = pick.reshape(3 * NF, 2, KE * P + NL)
    arrays["ident"] = np.eye(P, dtype=ml_dtypes.bfloat16)
    arrays["dense_t"] = np.concatenate([a["dense_ctx"].T, np.ones((1, BATCH), np.float32)])
    row = {pair: n for n, pair in enumerate((i, j) for i in range(NF) for j in range(i + 1, NF))}

    def w_row(i, j):
        f, g = ORDER[i], ORDER[j]
        return row[min(f, g), max(f, g)]

    w1 = np.zeros((KC * P, H1), np.float32)
    w1[:len(EARLY_PAIRS)] = a["W_top1"][[w_row(*q) for q in EARLY_PAIRS]]
    w1[KE * P:KE * P + NL] = a["W_top1"][[w_row(*q) for q in LATE_PAIRS]]
    w1[KE * P + NL:KC * P - 1] = a["W_top1"][len(row):]
    w1[KC * P - 1] = a["b_top1"]
    arrays["w1"] = np.ascontiguousarray(w1.reshape(KC, P, H1).transpose(1, 0, 2))
    arrays["w2"] = np.ascontiguousarray(a["W_top2"].reshape(N1, P, H2).transpose(1, 0, 2))
    arrays["b2"] = np.ascontiguousarray(a["b_top2"].reshape(N2, P).T)
    arrays["w3"] = np.ascontiguousarray(a["W_top3"].reshape(N2, P).T)

    nc = bacc.Bacc("TRN2", target_bir_lowering=False, num_devices=1)
    aps = {k: nc.dram_tensor(f"in_{k}", v.shape, mybir.dt.from_np(v.dtype), kind="ExternalInput").ap()
           for k, v in arrays.items()}
    out = nc.dram_tensor("out_y", (1, BATCH), mybir.dt.float32, kind="ExternalOutput").ap()
    big = [aps.pop(f"big{n}") for n in range(NB)]
    build_tower(nc, big=big, out=out, **aps)
    r = run_bass_kernel_spmd(nc, [{f"in_{k}": v for k, v in arrays.items()}], core_ids=[0])
    return r.results[0]["out_y"].reshape(BATCH, 1)
```

```python
import concourse.bass as bass
from concourse import mybir
from contextlib import ExitStack

P = 128
EMB = 64
BATCH = 512
NC = BATCH // P
ROWS = [125000, 125000, 1000, 125000, 1250, 1250, 12500, 12500, 1250, 1250, 1000, 1250, 12500, 12500, 12500,
        1000, 1250, 12500, 1000, 1250, 1000, 1250, 12500, 1000, 1000, 1000, 1250, 1250, 1000, 1000, 1000,
        1000, 1000, 1000, 1000, 1000, 1000, 1250, 1250]
NF = len(ROWS)
SMALL_ROWS = 1250
SMALL = sorted((f for f in range(NF) if ROWS[f] <= SMALL_ROWS), key=lambda f: ROWS[f])
BIG = [f for f in range(NF) if ROWS[f] > SMALL_ROWS]
NS, NB = len(SMALL), len(BIG)
BLOCKS = [-(-ROWS[f] // P) for f in SMALL]
BLOCK_AT = [sum(BLOCKS[:t]) for t in range(NS + 1)]
GROUPS = [(0, 4), (4, 8), (8, 12), (12, 17), (17, 21), (21, 25), (25, 29)]
NG = len(GROUPS)
LATE = 3
EARLY = NB - LATE
assert EARLY == NG and all(len({BLOCKS[t] for t in range(*g)}) == 1 for g in GROUPS)
ORDER = [f for g, (a, b) in enumerate(GROUPS) for f in SMALL[a:b] + [BIG[g]]] + BIG[EARLY:]
GROUP_AT = [a + g for g, (a, b) in enumerate(GROUPS)]
BIG_AT = [b + g for g, (a, b) in enumerate(GROUPS)]
NEARLY = NF - LATE
EARLY_PAIRS = [(i, j) for j in range(NEARLY) for i in range(j)]
LATE_PAIRS = [(i, j) for j in range(NEARLY, NF) for i in range(j)]
KE = -(-len(EARLY_PAIRS) // P)
KC = KE + 1
NL = len(LATE_PAIRS)
DENSE = 16
assert NL + DENSE + 1 == P
NEEDS = [max(j for _, j in EARLY_PAIRS[k * P:(k + 1) * P]) + 1 for k in range(KE)]
STAGES = [GROUP_AT[4] - 1, GROUP_AT[5] - 1, GROUP_AT[6] - 1, NEARLY]
STAGE_OF = [next(s for s, n in enumerate(STAGES) if n >= need) for need in NEEDS]
assert STAGE_OF == [0, 1, 2, 3, 3]
H1, H2 = 512, 256
N1, N2 = H1 // P, H2 // P
KINDS = 4
OCT = 8
NO = P // (KINDS * OCT)
FLIGHT = 3
HOT = 4


def build_tower(nc, ids_rows, ids_kinds, tables, big, kind_bits, kind_coef, pick, ident, dense_t, w1, w2, b2, w3, out):
    fp32, bf16, i32 = mybir.dt.float32, mybir.dt.bfloat16, mybir.dt.int32
    ALU = mybir.AluOpType
    ACT = mybir.ActivationFunctionType
    AX = mybir.AxisListType

    with ExitStack() as ctx:
        def sb(name, shape, dt):
            return ctx.enter_context(nc.sbuf_tensor(name, shape, dt))

        def ps(name, shape, dt):
            return ctx.enter_context(nc.psum_tensor(name, shape, dt))

        def sem(name):
            return ctx.enter_context(nc.semaphore(name))

        idr = sb("idr", [P, NC * NF], i32)
        idk = sb("idk", [P, BATCH], i32)
        tab = sb("tab", [P, BLOCK_AT[NS], EMB], fp32)
        cut = sb("cut", [P, 3 * BLOCK_AT[NS]], fp32)
        bits = sb("bits", [P, 3], i32)
        q = sb("q", [P, BATCH], i32)
        q2 = sb("q2", [P, BATCH], i32)
        q2_bits = sb("q2_bits", [P, BATCH], i32)
        q_bits = sb("q_bits", [P, BATCH], i32)
        kind = sb("kind", [P, BATCH], i32)
        kinds = sb("kinds", [P, NO, BATCH], bf16)
        coef = sb("coef", [P, OCT, P], bf16)
        hot = sb("hot", [P, NS, BATCH], bf16)
        blk = sb("blk", [P, NC, NS], i32)
        count = sb("count", [P, max(BLOCKS)], i32)
        mask = sb("mask", [P, NC * BLOCK_AT[NS]], bf16)
        prod = sb("prod", [P, 2, 512], fp32)
        row_e = sb("row_e", [P, EARLY, NC, EMB], fp32)
        row_l = sb("row_l", [P, NC, LATE, EMB], fp32)
        sums = sb("sums", [P, NC, 3, NF], fp32)
        sums_t = sb("sums_t", [3 * NF, NC, P], bf16)
        picks = sb("picks", [3 * NF, 2, KE * P + NL], bf16)
        idn = sb("idn", [P, P], bf16)
        first = sb("first", [P, 2, BATCH], fp32)
        z = sb("z", [P, KC, BATCH], fp32)
        w1s = sb("w1s", [P, KC, H1], fp32)
        w2s = sb("w2s", [P, N1, H2], fp32)
        w3s = sb("w3s", [P, N2], fp32)
        b2s = sb("b2s", [P, N2], fp32)
        h1 = sb("h1", [P, N1, BATCH], fp32)
        h2 = sb("h2", [P, N2, BATCH], fp32)
        y = sb("y", [P, NC], fp32)
        warm = sb("warm", [P, 1], fp32)

        acc = ps("acc", [P, N1, BATCH], fp32)
        pk0 = ps("pk0", [P, 512], fp32)
        pk1 = ps("pk1", [P, 512], fp32)
        fa = ps("fa", [P, 512], fp32)
        fb = ps("fb", [P, 512], fp32)
        pk = [pk0, pk1]
        FIRST, SECOND, TURNED = slice(0, P), slice(P, 2 * P), slice(2 * P, 2 * P + P // 2)
        late = [(fa, fb)[c % 2] for c in range(NC)]

        ids_rows_in, ids_kinds_in, bits_in, coef_in = (sem(n) for n in ("ids_rows_in", "ids_kinds_in", "bits_in", "coef_in"))
        table_in = [sem(f"table_in{n}") for n in range(2 * NG)]
        early_in = [sem(f"early_in{n}") for n in range(EARLY)]
        late_in = [sem(f"late_in{c}") for c in range(NC)]
        picks_in, ident_in, dense_in = sem("picks_in"), sem("ident_in"), sem("dense_in")
        w1_in = [sem(f"w1_in{k}") for k in range(KC)]
        w2_in, tail_in = sem("w2_in"), sem("tail_in")
        cleared = sem("cleared")
        zeroed = sem("zeroed")
        kind_ready = sem("kind_ready")
        kinds_ready = sem("kinds_ready")
        arg_ready = sem("arg_ready")
        hot_ready = sem("hot_ready")
        cut_ready = sem("cut_ready")
        picked = sem("picked")
        mask_ready = sem("mask_ready")
        masked = sem("masked")
        sums_ready = sem("sums_ready")
        turned = sem("turned")
        sums_t_ready = sem("sums_t_ready")
        factors = sem("factors")
        first_ready = sem("first_ready")
        z_ready = sem("z_ready")
        layer1 = sem("layer1")
        h1_ready = sem("h1_ready")
        layer2 = [sem(f"layer2_{m}") for m in range(N2)]
        h2_ready = [sem(f"h2_ready_{m}") for m in range(N2)]
        layer3_done = sem("layer3_done")
        y_ready = sem("y_ready")
        y_out = sem("y_out")
        dve_step = sem("dve_step")

        def upper(ap):
            names = " ".join("abcd"[:len(ap.shape) - 1])
            halves_of = ap.bitcast(bf16).rearrange(f"{names} (y u) -> {names} y u", u=2)
            return halves_of[(slice(None),) * len(ap.shape) + (1,)]

        def cut_of(a, b, part):
            n = BLOCKS[a]
            return cut[:, 3 * BLOCK_AT[a]:3 * BLOCK_AT[b]].rearrange(
                "p (t k j) -> p t k j", k=3, j=n)[:, :, part, :]

        def mask_of(g):
            a, b = GROUPS[g]
            return mask[:, NC * BLOCK_AT[a]:NC * BLOCK_AT[b]]

        halves = [((a, a + 2), (a + 2, b)) for a, b in GROUPS]
        block = ctx.enter_context(nc.Block())

        @block.sync
        def _(sp):
            def load_tables(n):
                a, b = halves[n // 2][n % 2]
                if n >= FLIGHT:
                    sp.wait_ge(table_in[n - FLIGHT], 16)
                sp.dma_start(tab[:, BLOCK_AT[a]:BLOCK_AT[b], :],
                             tables[:, BLOCK_AT[a]:BLOCK_AT[b], :]).then_inc(table_in[n], 16)

            sp.dma_start(idr[:, :], ids_rows).then_inc(ids_rows_in, 16)
            load_tables(0)
            sp.dma_start(coef[:, :, :], kind_coef).then_inc(coef_in, 16)
            for n in range(1, 2 * NG):
                load_tables(n)
                if n == 6:
                    sp.dma_start(picks[:, :, :], pick).then_inc(picks_in, 16)
                    sp.dma_start(idn[:, :], ident).then_inc(ident_in, 16)
                if n >= 7 and n % 2:
                    k = (n - 7) // 2
                    sp.dma_start(w1s[:, k, :], w1[:, k, :]).then_inc(w1_in[k], 16)
            for k in range(4, KC):
                sp.dma_start(w1s[:, k, :], w1[:, k, :]).then_inc(w1_in[k], 16)
            sp.dma_start(z[NL:P, KE, :], dense_t).then_inc(dense_in, 16)
            sp.dma_start(w2s[:, :, :], w2).then_inc(w2_in, 16)
            sp.dma_start(w3s[:, :], w3).then_inc(tail_in, 16)
            sp.dma_start(b2s[:, :], b2).then_inc(tail_in, 16)
            sp.wait_ge(y_ready, 1)
            sp.dma_start(out, y[:, :]).then_inc(y_out, 16)
            sp.wait_ge(y_out, 16)

        @block.gpsimd
        def _(pool):
            nc.gpsimd.iota(count[:, :], pattern=[[1, max(BLOCKS)]], base=0, channel_multiplier=0).then_inc(cleared, 1)
            nc.gpsimd.memset(sums[:, :, :, :], 0.0).then_inc(cleared, 1)
            pool.wait_ge(ids_rows_in, 16)

            def gather(rows, n, c, done):
                at = c * NF + NS + n
                pool.indirect_dma_start(
                    out=rows, out_offset=None, in_=big[n][:, :],
                    in_offset=bass.IndirectOffsetOnAxis(ap=idr[:, at:at + 1], axis=0)).then_inc(done, 16)

            for n in range(EARLY):
                for c in range(NC):
                    gather(row_e[:, n, c, :], n, c, early_in[n])
            for c in range(NC):
                for n in range(LATE):
                    gather(row_l[:, c, n, :], EARLY + n, c, late_in[c])

        @block.scalar
        def _(act):
            act.dma_start(idk[:, :], ids_kinds).then_inc(ids_kinds_in, 16)
            act.dma_start(bits[:, :], kind_bits).then_inc(bits_in, 16)
            act.wait_ge(cleared, 2)
            nc.scalar.activation(warm[:, :], sums[:, 0, 0, 0:1], ACT.Relu)
            act.wait_ge(zeroed, 1)
            act.wait_ge(kind_ready, 1)
            for o in range(NO):
                rows = slice(P // NO * o, P // NO * (o + 1))
                nc.scalar.activation(kinds[rows, o, :], kind[rows, :], ACT.Copy).then_inc(kinds_ready, 1)
            for t in range(NS):
                act.wait_ge(arg_ready, t + 1)
                nc.scalar.activation(hot[:, t, :], acc[:, t % HOT, :], ACT.Relu).then_inc(hot_ready, 1)

            for s in range(len(STAGES)):
                act.wait_ge(turned, s + 1)
                nc.scalar.activation(sums_t[:, :, :], fa[0:3 * NF, 0:BATCH // 2].bitcast(bf16).rearrange(
                    "p (c x) -> p c x", x=P), ACT.Copy).then_inc(sums_t_ready, 1)
                for k in range(KE):
                    if STAGE_OF[k] == s:
                        act.wait_ge(factors, k + 1)
                        if k >= 2:
                            act.wait_ge(z_ready, k - 1)
                        nc.scalar.activation(first[:, k % 2, :], fa[:, :], ACT.Copy).then_inc(first_ready, 1)
            act.wait_ge(tail_in, 32)

            def sums_t_late(c):
                act.wait_ge(turned, len(STAGES) + c + 1)
                nc.scalar.activation(sums_t[:, c, :], late[c][0:3 * NF, TURNED].bitcast(bf16),
                                     ACT.Copy).then_inc(sums_t_ready, 1)

            def first_late(c):
                k = KE + c
                act.wait_ge(factors, k + 1)
                act.wait_ge(z_ready, k - 1)
                nc.scalar.activation(first[0:NL, k % 2, 0:P], late[c][0:NL, FIRST], ACT.Copy).then_inc(first_ready, 1)

            def relu1(c):
                act.wait_ge(layer1, c + 1)
                nc.scalar.activation(h1[:, :, c * P:(c + 1) * P], acc[:, :, c * P:(c + 1) * P],
                                     ACT.Relu).then_inc(h1_ready, 1)

            def relu2(c):
                act.wait_ge(layer2[1], c + 1)
                nc.scalar.activation(h2[:, 1, c * P:(c + 1) * P], pk1[:, 0:P], ACT.Relu,
                                     bias=b2s[:, 1:2]).then_inc(h2_ready[1], 1)

            sums_t_late(0)
            first_late(0)
            relu1(0)
            sums_t_late(1)
            first_late(1)
            for c in range(1, NC):
                relu1(c)
                if c + 1 < NC:
                    sums_t_late(c + 1)
                relu2(c - 1)
                if c + 1 < NC:
                    first_late(c + 1)
            relu2(NC - 1)

        @block.vector
        def _(dve):
            steps = [0]

            def mark(ins):
                steps[0] += 1
                ins.then_inc(dve_step, 1)
                return steps[0]

            def after(step):
                dve.wait_ge(dve_step, step)

            nc.vector.memset(kinds[:, :, :].bitcast(fp32), 0.0).then_inc(zeroed, 1)
            dve.wait_ge(ids_kinds_in, 16)
            dve.wait_ge(bits_in, 16)
            have_q = mark(nc.vector.tensor_single_scalar(q[:, :], idk[:, :], P - 1, ALU.bitwise_and))
            nc.vector.tensor_scalar(q_bits[:, :], idk[:, :], bits[:, 0:1], bits[:, 2:3], ALU.bitwise_and, ALU.bitwise_or)
            after(have_q)
            after(mark(nc.vector.tensor_tensor(q2[:, :], q[:, :], q[:, :], ALU.mult)))
            after(mark(nc.vector.tensor_scalar(q2_bits[:, :], q2[:, :], bits[:, 1:2], None, ALU.bitwise_and)))
            nc.vector.tensor_tensor(kind[:, :], q_bits[:, :], q2_bits[:, :], ALU.bitwise_or).then_inc(kind_ready, 1)
            dve.wait_ge(ids_rows_in, 16)
            dve.wait_ge(cleared, 2)
            after(mark(nc.vector.tensor_single_scalar(
                blk[:, :, :], idr[:, :].rearrange("p (c f) -> p c f", c=NC)[:, :, 0:NS], 7, ALU.arith_shift_right)))

            def masks(g):
                a, b = GROUPS[g]
                n = BLOCKS[a]
                nc.vector.tensor_tensor(
                    mask_of(g).rearrange("p (c t j) -> p c t j", c=NC, j=n),
                    blk[:, :, a:b].unsqueeze(3).to_broadcast([P, NC, b - a, n]),
                    count[:, 0:n].unsqueeze(1).unsqueeze(1).to_broadcast([P, NC, b - a, n]),
                    ALU.is_equal).then_inc(mask_ready, 1)

            def row_sums(g, n):
                a, b = halves[g][n]
                dve.wait_ge(table_in[2 * g + n], 16)
                return mark(nc.vector.tensor_reduce(
                    cut_of(a, b, 0), tab[:, BLOCK_AT[a]:BLOCK_AT[b], :].rearrange("p (t j) x -> p t j x", j=BLOCKS[a]),
                    axis=AX.X, op=ALU.add))

            def cut_rows(g, part):
                a, b = GROUPS[g]
                return nc.vector.tensor_tensor(cut_of(a, b, part), cut_of(a, b, part - 1),
                                               upper(cut_of(a, b, part - 1)), ALU.subtract)

            def mask_blocks(g):
                a, b = GROUPS[g]
                n, w = BLOCKS[a], NC * (BLOCK_AT[b] - BLOCK_AT[a])
                dve.wait_ge(picked, g + 1)
                dve.wait_ge(mask_ready, g + 1)
                nc.vector.tensor_tensor(prod[:, g % 2, 0:w], pk[g % 2][:, 0:w], mask_of(g),
                                        ALU.mult).then_inc(masked, 1)

            def add_blocks(g):
                a, b = GROUPS[g]
                n, w = BLOCKS[a], NC * (BLOCK_AT[b] - BLOCK_AT[a])
                dve.wait_ge(masked, g + 1)
                return mark(nc.vector.tensor_reduce(
                    sums[:, :, 0, GROUP_AT[g]:GROUP_AT[g] + b - a],
                    prod[:, g % 2, 0:w].rearrange("p (c t j) -> p c t j", c=NC, j=n), axis=AX.X, op=ALU.add))

            def big_sums(n):
                dve.wait_ge(early_in[n], 16 * NC)
                return mark(nc.vector.tensor_reduce(sums[:, :, 0, BIG_AT[n]:BIG_AT[n] + 1], row_e[:, n, :, :],
                                                    axis=AX.X, op=ALU.add))

            def cut_stage(s, part):
                lo, hi = ([0] + STAGES)[s], STAGES[s]
                return nc.vector.tensor_tensor(sums[:, :, part, lo:hi], sums[:, :, part - 1, lo:hi],
                                               upper(sums[:, :, part - 1, lo:hi]), ALU.subtract)

            def products(k):
                dve.wait_ge(first_ready, k + 1)
                nc.vector.tensor_tensor(z[:, k, :], first[:, k % 2, :], fb[:, :], ALU.mult).then_inc(z_ready, 1)

            for g in range(NG):
                if g == 0:
                    masks(0)
                row_sums(g, 0)
                if g >= 1:
                    s = g - 4
                    if s >= 1:
                        dve.wait_ge(turned, s)
                    mask_blocks(g - 1)
                    if g == 1:
                        masks(1)
                    if g < NG - 1:
                        masks(g + 1)
                    added = add_blocks(g - 1)
                    if s >= 1:
                        products(s - 1)
                    if g >= 2:
                        added = big_sums(g - 2)
                    if s >= 0:
                        after(added)
                        after(mark(cut_stage(s, 1)))
                        cut_stage(s, 2).then_inc(sums_ready, 1)
                after(row_sums(g, 1))
                after(mark(cut_rows(g, 1)))
                cut_rows(g, 2).then_inc(cut_ready, 1)
            dve.wait_ge(turned, 3)
            big_sums(5)
            products(2)
            mask_blocks(6)
            big_sums(6)
            after(add_blocks(6))
            after(mark(cut_stage(3, 1)))
            cut_stage(3, 2).then_inc(sums_ready, 1)
            products(3)
            products(4)
            dve.wait_ge(tail_in, 32)
            dve.wait_ge(turned, len(STAGES))

            def late_sums(c):
                dve.wait_ge(late_in[c], 16 * LATE)
                after(mark(nc.vector.tensor_reduce(sums[:, c, 0, NEARLY:NF], row_l[:, c, :, :],
                                                   axis=AX.X, op=ALU.add)))
                after(mark(nc.vector.tensor_tensor(sums[:, c, 1, NEARLY:NF], sums[:, c, 0, NEARLY:NF],
                                                   upper(sums[:, c, 0, NEARLY:NF]), ALU.subtract)))
                nc.vector.tensor_tensor(sums[:, c, 2, NEARLY:NF], sums[:, c, 1, NEARLY:NF],
                                        upper(sums[:, c, 1, NEARLY:NF]), ALU.subtract).then_inc(sums_ready, 1)

            def late_products(c):
                dve.wait_ge(first_ready, KE + c + 1)
                nc.vector.tensor_tensor(z[0:NL, KE, c * P:(c + 1) * P], first[0:NL, (KE + c) % 2, 0:P],
                                        late[c][0:NL, SECOND], ALU.mult).then_inc(z_ready, 1)

            def relu2(c):
                dve.wait_ge(layer2[0], c + 1)
                nc.vector.tensor_scalar(h2[:, 0, c * P:(c + 1) * P], pk0[:, 0:P], b2s[:, 0:1], 0.0,
                                        ALU.add, ALU.max).then_inc(h2_ready[0], 1)

            for c in range(NC):
                late_sums(c)
                if c >= 2:
                    relu2(c - 2)
                late_products(c)
            relu2(NC - 2)
            relu2(NC - 1)
            dve.wait_ge(layer3_done, 1)
            nc.vector.tensor_copy(y[:, :], pk0[:, 2 * P:2 * P + NC]).then_inc(y_ready, 1)

        @block.tensor
        def _(pe):
            def hot_arg(t):
                if t >= HOT:
                    pe.wait_ge(hot_ready, t - HOT + 1)
                pe.wait_ge(kinds_ready, t // OCT + 1)
                nc.tensor.matmul(acc[:, t % HOT, :], coef[:, t % OCT, :], kinds[:, t // OCT, :],
                                 start=True, stop=True).then_inc(arg_ready, 1)

            def pick_rows(g):
                a, b = GROUPS[g]
                n, w = BLOCKS[a], b - a
                pe.wait_ge(cut_ready, g + 1)
                pe.wait_ge(hot_ready, b)
                if g >= 2:
                    pe.wait_ge(masked, g - 1)
                for c in range(NC):
                    for t in range(a, b):
                        at = (c * w + t - a) * n
                        for part in range(3):
                            last = nc.tensor.matmul(pk[g % 2][:, at:at + n], hot[:, t, c * P:(c + 1) * P],
                                                    upper(cut_of(t, t + 1, part)[:, 0, :]),
                                                    start=(part == 0), stop=(part == 2))
                last.then_inc(picked, 1)

            def turn_sums(s):
                pe.wait_ge(sums_ready, s + 1)
                if s >= 1:
                    pe.wait_ge(first_ready, s)
                for c in range(NC):
                    last = nc.tensor.transpose(fa[0:3 * NF, c * P // 2:(c + 1) * P // 2].bitcast(bf16),
                                               upper(sums[:, c, :, :].rearrange("p k f -> p (k f)")), idn[:, :])
                last.then_inc(turned, 1)

            def early_factors(k):
                pe.wait_ge(sums_t_ready, STAGE_OF[k] + 1)
                if k >= 1:
                    pe.wait_ge(z_ready, k)
                for side, bank in ((0, fa), (1, fb)):
                    last = nc.tensor.matmul(bank[:, :], picks[:, side, k * P:(k + 1) * P], sums_t[:, :, :],
                                            start=True, stop=True)
                last.then_inc(factors, 1)

            def layer1_early(k, ns=range(N1)):
                pe.wait_ge(w1_in[k], 16)
                pe.wait_ge(z_ready, k + 1)
                for n in ns:
                    nc.tensor.matmul(acc[:, n, :], w1s[:, k, n * P:(n + 1) * P], z[:, k, :],
                                     start=(k == 0), stop=False, skip_group_check=True)

            def turn_late(c):
                pe.wait_ge(sums_ready, len(STAGES) + c + 1)
                pe.wait_ge(z_ready, KE + max(c - 1, 0))
                nc.tensor.transpose(late[c][0:3 * NF, TURNED].bitcast(bf16),
                                    upper(sums[:, c, :, :].rearrange("p k f -> p (k f)")), idn[:, :]).then_inc(turned, 1)

            def late_factors(c):
                pe.wait_ge(sums_t_ready, len(STAGES) + c + 1)
                for side, part in ((0, FIRST), (1, SECOND)):
                    last = nc.tensor.matmul(late[c][0:NL, part], picks[:, side, KE * P:KE * P + NL], sums_t[:, c, :],
                                            start=True, stop=True)
                last.then_inc(factors, 1)

            def layer1_late(c):
                pe.wait_ge(z_ready, KE + c + 1)
                for n in range(N1):
                    last = nc.tensor.matmul(acc[:, n, c * P:(c + 1) * P], w1s[:, KE, n * P:(n + 1) * P],
                                            z[:, KE, c * P:(c + 1) * P], start=False, stop=True,
                                            skip_group_check=True)
                last.then_inc(layer1, 1)

            def layer2_half(c, m):
                if m == 0:
                    pe.wait_ge(h1_ready, c + 1)
                if c >= 1:
                    pe.wait_ge(h2_ready[m], c)
                for n in range(N1):
                    last = nc.tensor.matmul(pk[m][:, 0:P], w2s[:, n, m * P:(m + 1) * P],
                                            h1[:, n, c * P:(c + 1) * P], start=(n == 0), stop=(n == N1 - 1))
                last.then_inc(layer2[m], 1)

            def layer3(c):
                for m in range(N2):
                    pe.wait_ge(h2_ready[m], c + 1)
                    last = nc.tensor.matmul(pk0[:, 2 * P + c:2 * P + c + 1], h2[:, m, c * P:(c + 1) * P],
                                            w3s[:, m:m + 1], start=(m == 0), stop=(m == N2 - 1))
                return last

            pe.wait_ge(coef_in, 16)
            ahead = [6, 14, 22, NS]
            for g in range(NG):
                if g < len(ahead):
                    for t in range(([0] + ahead)[g], ahead[g]):
                        hot_arg(t)
                pick_rows(g)
                if g == 3:
                    pe.wait_ge(ident_in, 16)
                    pe.wait_ge(picks_in, 16)
                if g == 4:
                    pe.wait_ge(hot_ready, NS)
                if g >= 4:
                    turn_sums(g - 4)
                    early_factors(g - 4)
                    if g >= 5:
                        layer1_early(g - 5)
            turn_sums(3)
            early_factors(3)
            layer1_early(2)
            early_factors(4)
            layer1_early(3)
            turn_late(0)
            layer1_early(4, range(N1 // 2))
            late_factors(0)
            layer1_early(4, range(N1 // 2, N1))
            pe.wait_ge(w1_in[KE], 16)
            pe.wait_ge(dense_in, 16)
            pe.wait_ge(w2_in, 16)
            pe.wait_ge(tail_in, 32)
            layer1_late(0)
            turn_late(1)
            late_factors(1)
            for c in range(1, NC):
                layer2_half(c - 1, 0)
                layer1_late(c)
                if c + 1 < NC:
                    turn_late(c + 1)
                layer2_half(c - 1, 1)
                if c + 1 < NC:
                    late_factors(c + 1)
                layer3(c - 1)
            layer2_half(NC - 1, 0)
            layer2_half(NC - 1, 1)
            layer3(NC - 1).then_inc(layer3_done, 1)


def kernel(**inputs):
    import ml_dtypes
    import numpy as np
    import concourse.bacc as bacc
    from concourse.bass_utils import run_bass_kernel_spmd

    a = {k: np.asarray(v) for k, v in inputs.items()}
    ids = a["ids"]
    arrays = {}
    arrays["ids_rows"] = np.ascontiguousarray(
        ids[:, SMALL + BIG].reshape(NC, P, NF).transpose(1, 0, 2).reshape(P, NC * NF))
    cols = np.zeros((NO * OCT, BATCH), ids.dtype)
    cols[:NS] = ids[:, SMALL].T
    arrays["ids_kinds"] = np.repeat(cols.reshape(NO, 1, OCT, BATCH), KINDS, axis=1).reshape(P, BATCH)
    tables = np.zeros((P, BLOCK_AT[NS], EMB), np.float32)
    for t, f in enumerate(SMALL):
        padded = np.zeros((BLOCKS[t] * P, EMB), np.float32)
        padded[:ROWS[f]] = a[f"tbl_{f}"]
        tables[:, BLOCK_AT[t]:BLOCK_AT[t + 1]] = padded.reshape(BLOCKS[t], P, EMB).transpose(1, 0, 2)
    arrays["tables"] = tables
    for n, f in enumerate(BIG):
        arrays[f"big{n}"] = np.ascontiguousarray(a[f"tbl_{f}"])
    bits = np.array([[P - 1, 0, 0], [0, P * P - P, 0], [0, P - 1, 0], [0, 0, 1]], np.int32)
    arrays["kind_bits"] = np.tile(np.repeat(bits, OCT, axis=0), (NO, 1))
    p = np.arange(P)
    coef = np.zeros((KINDS, OCT, OCT, P), ml_dtypes.bfloat16)
    for i in range(OCT):
        coef[0, i, i] = 2 * p
        coef[1, i, i] = coef[2, i, i] = -1
        coef[3, i, i] = (1 - p * p) // P * P
        coef[3, (i + 1) % OCT, i] = (1 - p * p) % P
    arrays["kind_coef"] = np.tile(coef.reshape(KINDS * OCT, OCT, P), (NO, 1, 1))
    pick = np.zeros((3, NF, 2, KE * P + NL), ml_dtypes.bfloat16)
    for at, pairs in ((0, EARLY_PAIRS), (KE * P, LATE_PAIRS)):
        for n, (i, j) in enumerate(pairs):
            pick[:, i, 0, at + n] = 1
            pick[:, j, 1, at + n] = 1
    arrays["pick"] = pick.reshape(3 * NF, 2, KE * P + NL)
    arrays["ident"] = np.eye(P, dtype=ml_dtypes.bfloat16)
    arrays["dense_t"] = np.concatenate([a["dense_ctx"].T, np.ones((1, BATCH), np.float32)])
    row = {pair: n for n, pair in enumerate((i, j) for i in range(NF) for j in range(i + 1, NF))}

    def w_row(i, j):
        f, g = ORDER[i], ORDER[j]
        return row[min(f, g), max(f, g)]

    w1 = np.zeros((KC * P, H1), np.float32)
    w1[:len(EARLY_PAIRS)] = a["W_top1"][[w_row(*q) for q in EARLY_PAIRS]]
    w1[KE * P:KE * P + NL] = a["W_top1"][[w_row(*q) for q in LATE_PAIRS]]
    w1[KE * P + NL:KC * P - 1] = a["W_top1"][len(row):]
    w1[KC * P - 1] = a["b_top1"]
    arrays["w1"] = np.ascontiguousarray(w1.reshape(KC, P, H1).transpose(1, 0, 2))
    arrays["w2"] = np.ascontiguousarray(a["W_top2"].reshape(N1, P, H2).transpose(1, 0, 2))
    arrays["b2"] = np.ascontiguousarray(a["b_top2"].reshape(N2, P).T)
    arrays["w3"] = np.ascontiguousarray(a["W_top3"].reshape(N2, P).T)

    nc = bacc.Bacc("TRN2", target_bir_lowering=False, num_devices=1)
    aps = {k: nc.dram_tensor(f"in_{k}", v.shape, mybir.dt.from_np(v.dtype), kind="ExternalInput").ap()
           for k, v in arrays.items()}
    out = nc.dram_tensor("out_y", (P, NC), mybir.dt.float32, kind="ExternalOutput").ap()
    big = [aps.pop(f"big{n}") for n in range(NB)]
    build_tower(nc, big=big, out=out, **aps)
    r = run_bass_kernel_spmd(nc, [{f"in_{k}": v for k, v in arrays.items()}], core_ids=[0])
    return np.ascontiguousarray(r.results[0]["out_y"].T).reshape(BATCH, 1)
```

```python
import concourse.bass as bass
from concourse import mybir
from contextlib import ExitStack

P = 128
EMB = 64
BATCH = 512
NC = BATCH // P
ROWS = [125000, 125000, 1000, 125000, 1250, 1250, 12500, 12500, 1250, 1250, 1000, 1250, 12500, 12500, 12500,
        1000, 1250, 12500, 1000, 1250, 1000, 1250, 12500, 1000, 1000, 1000, 1250, 1250, 1000, 1000, 1000,
        1000, 1000, 1000, 1000, 1000, 1000, 1250, 1250]
NF = len(ROWS)
NS = 28
SMALL = sorted(range(NF), key=lambda f: ROWS[f])[1:1 + NS]
BIG = [f for f in range(NF) if f not in SMALL]
NB = len(BIG)
BLOCKS = [-(-ROWS[f] // P) for f in SMALL]
BLOCK_AT = [sum(BLOCKS[:t]) for t in range(NS + 1)]
MAXB = max(BLOCKS)
LANE = 32
GROUPS = [(t, t + P // LANE) for t in range(0, NS, P // LANE)]
NG = len(GROUPS)
assert 3 * MAXB <= LANE and all(BLOCKS[a] == BLOCKS[b - 1] for a, b in GROUPS)
LATE = 3
EARLY = NB - LATE
assert EARLY == NG + 1
ORDER = [f for g, (a, b) in enumerate(GROUPS) for f in SMALL[a:b] + (BIG[g - 1:g] if g else [])] + BIG[NG - 1:]
BIG_AT = [ORDER.index(f) for f in BIG[:EARLY]]
NEARLY = NF - LATE
ROWS_T = LANE + 3 * NS
assert 3 * EARLY <= LANE and ROWS_T <= P
EARLY_PAIRS = [(i, j) for j in range(NEARLY) for i in range(j)]
LATE_PAIRS = [(i, j) for j in range(NEARLY, NF) for i in range(j)]
KE = -(-len(EARLY_PAIRS) // P)
KC = KE + 1
NL = len(LATE_PAIRS)
DENSE = 16
assert NL + DENSE + 1 == P
NEEDS = [max(j for _, j in EARLY_PAIRS[k * P:(k + 1) * P]) + 1 for k in range(KE)]
FIRST_STAGE = 3
STAGES = [BIG_AT[g - 1] + 1 for g in range(FIRST_STAGE, NG)] + [NEARLY]
assert len(STAGES) == KE and all(need <= known for need, known in zip(NEEDS, STAGES))
HALF = BATCH // 2
NH = BATCH // HALF
H1, H2 = 512, 256
N1, N2 = H1 // P, H2 // P
KINDS = 4
HIGH, LOW = 120, 7
BLOCK = 1920
HIGH_1, LOW_1, BLOCK_1 = 8, 1, 128
SLOTS = 8
OCT = SLOTS - 1
NO = P // (KINDS * SLOTS)
assert NO * OCT == NS and (max(ROWS[f] for f in SMALL) - 1) // P * P <= BLOCK
PAIR = 2
KINDS_AFTER = [2, 8, 18]
BANKS = 4
AHEAD = [10, 16, 24, 31, 35]
FLIGHT = 2


def build_tower(nc, ids_rows, ids_kinds, tables, big, digit_consts, digit_coef, block_coef, lanes, pick,
                pick_late, ident, dense_t, w1, w2, b2, w3, out):
    fp32, bf16, i32 = mybir.dt.float32, mybir.dt.bfloat16, mybir.dt.int32
    ALU = mybir.AluOpType
    ACT = mybir.ActivationFunctionType
    AX = mybir.AxisListType

    with ExitStack() as ctx:
        def sb(name, shape, dt):
            return ctx.enter_context(nc.sbuf_tensor(name, shape, dt))

        def ps(name, shape, dt):
            return ctx.enter_context(nc.psum_tensor(name, shape, dt))

        def sem(name):
            return ctx.enter_context(nc.semaphore(name))

        idr = sb("idr", [P, NC * NF], i32)
        idk = sb("idk", [P, BATCH], i32)
        consts = sb("consts", [P, 4], i32)
        step = consts[:, 2:4].bitcast(fp32)
        digit = sb("digit", [P, 2, BATCH], i32)
        kinds = sb("kinds", [P, NO, BATCH], bf16)
        block_kinds = sb("block_kinds", [P, BATCH], bf16)
        coef = sb("coef", [P, OCT, P], bf16)
        bcoef = sb("bcoef", [P, NG, P], bf16)
        onehot = sb("onehot", [P, NS + NG, BATCH], bf16)
        tab = sb("tab", [P, BLOCK_AT[NS], EMB], fp32)
        cut = sb("cut", [P, NS, LANE], fp32)
        kept = sb("kept", [P, 2, BATCH], bf16)
        lane_sum = sb("lane_sum", [P, ROWS_T + NS - P // LANE], bf16)
        row_e = sb("row_e", [P, EARLY, NC, EMB], fp32)
        row_l = sb("row_l", [P, NC, LATE, EMB], fp32)
        sums_e = sb("sums_e", [P, NC, LANE], fp32)
        sums_l = sb("sums_l", [P, NC, 3, LATE], fp32)
        sums_t = sb("sums_t", [ROWS_T, BATCH], bf16)
        sums_lt = sb("sums_lt", [3 * LATE, BATCH], bf16)
        picks = sb("picks", [ROWS_T, KC, 2, P], bf16)
        picks_l = sb("picks_l", [3 * LATE, 2, NL], bf16)
        idn = sb("idn", [P, P], bf16)
        first = sb("first", [P, 2, BATCH], fp32)
        z = sb("z", [P, KC, BATCH], fp32)
        w1s = sb("w1s", [P, KC, H1], fp32)
        w2s = sb("w2s", [P, N1, H2], fp32)
        w3s = sb("w3s", [P, N2], fp32)
        b2s = sb("b2s", [P, N2], fp32)
        h1 = sb("h1", [P, N1, BATCH], fp32)
        h2 = sb("h2", [P, N2, BATCH], fp32)
        y = sb("y", [P, NC], fp32)
        warm = sb("warm", [P, 2], fp32)
        idle = sb("idle", [P, BATCH], bf16)

        acc = ps("acc", [P, N1, BATCH], fp32)
        pk = ps("pk", [P, BATCH], fp32)
        st = ps("st", [P, BATCH], fp32)
        fa = ps("fa", [P, BATCH], fp32)
        fb = ps("fb", [P, BATCH], fp32)
        l2 = [pk, st]
        late_t = fb[0:3 * LATE, 0:BATCH // 2].bitcast(bf16)

        ids_rows_in, ids_kinds_in, consts_in, coef_in, bcoef_in = (
            sem(n) for n in ("ids_rows_in", "ids_kinds_in", "consts_in", "coef_in", "bcoef_in"))
        table_in = [sem(f"table_in{n}") for n in range(2 * NG)]
        early_in = [sem(f"early_in{n}") for n in range(EARLY)]
        late_in = [sem(f"late_in{c}") for c in range(NC)]
        lanes_in, picks_in, ident_in, dense_in = sem("lanes_in"), sem("picks_in"), sem("ident_in"), sem("dense_in")
        picks_rest_in = sem("picks_rest_in")
        w1_in = [sem(f"w1_in{k}") for k in range(KC)]
        w2_in, tail_in = sem("w2_in"), sem("tail_in")
        warm_zeroed = sem("warm_zeroed")
        idle_ready = sem("idle_ready")
        lanes_zeroed = sem("lanes_zeroed")
        kinds_zeroed = sem("kinds_zeroed")
        sums_zeroed = sem("sums_zeroed")
        digits_ready = sem("digits_ready")
        kinds_ready = sem("kinds_ready")
        block_kinds_ready = sem("block_kinds_ready")
        arg_ready = sem("arg_ready")
        first_pair_ready = sem("first_pair_ready")
        onehot_ready = sem("onehot_ready")
        cut_ready = sem("cut_ready")
        picked = sem("picked")
        kept_ready = sem("kept_ready")
        summed = sem("summed")
        big_ready = sem("big_ready")
        turned = sem("turned")
        sums_t_ready = sem("sums_t_ready")
        factors = sem("factors")
        first_ready = sem("first_ready")
        z_ready = sem("z_ready")
        layer1 = sem("layer1")
        h1_ready = sem("h1_ready")
        layer2 = [sem(f"layer2_{m}") for m in range(N2)]
        h2_ready = [sem(f"h2_ready_{m}") for m in range(N2)]
        layer3_done = sem("layer3_done")
        y_ready = sem("y_ready")
        y_out = sem("y_out")
        dve_step = sem("dve_step")

        def upper(ap):
            names = " ".join("abcd"[:len(ap.shape) - 1])
            halves_of = ap.bitcast(bf16).rearrange(f"{names} (y u) -> {names} y u", u=2)
            return halves_of[(slice(None),) * len(ap.shape) + (1,)]

        def cut_of(a, b, part):
            return cut[:, a:b, part * MAXB:part * MAXB + BLOCKS[a]]

        def hot_number(g, t):
            return t + g

        def mask_number(g):
            return GROUPS[g][1] + g

        def wait_onehot(engine, number):
            if number < PAIR:
                engine.wait_ge(first_pair_ready, 1)
            else:
                engine.wait_ge(onehot_ready, number // PAIR)

        halves = [((a, a + 2), (a + 2, b)) for a, b in GROUPS]
        block = ctx.enter_context(nc.Block())

        @block.sync
        def _(sp):
            def load_tables(n):
                a, b = halves[n // 2][n % 2]
                if n >= FLIGHT:
                    sp.wait_ge(table_in[n - FLIGHT], 16)
                sp.dma_start(tab[:, BLOCK_AT[a]:BLOCK_AT[b], :],
                             tables[:, BLOCK_AT[a]:BLOCK_AT[b], :]).then_inc(table_in[n], 16)

            def load_w1(k):
                sp.dma_start(w1s[:, k, :], w1[:, k, :]).then_inc(w1_in[k], 16)

            sp.dma_start(idk[:, :], ids_kinds).then_inc(ids_kinds_in, 16)
            sp.dma_start(idr[:, :], ids_rows).then_inc(ids_rows_in, 16)
            sp.dma_start(coef[:, :, :], digit_coef).then_inc(coef_in, 16)
            for n in range(2 * NG):
                load_tables(n)
                if n == 0:
                    sp.dma_start(bcoef[:, :, :], block_coef).then_inc(bcoef_in, 16)
                if n == 3:
                    sp.dma_start(lane_sum[:, :], lanes).then_inc(lanes_in, 16)
                if n == 6:
                    sp.dma_start(idn[:, :], ident).then_inc(ident_in, 16)
                    sp.dma_start(picks[:, 0:3, :, :], pick[:, 0:3, :, :]).then_inc(picks_in, 16)
                    sp.dma_start(picks_l[:, :, :], pick_late).then_inc(picks_in, 16)
                if n == 9:
                    load_w1(0)
                if n == 12:
                    load_w1(1)
            sp.dma_start(picks[:, 3:KC, :, :], pick[:, 3:KC, :, :]).then_inc(picks_rest_in, 16)
            for k in range(2, KC):
                load_w1(k)
            sp.dma_start(z[NL:P, KE, :], dense_t).then_inc(dense_in, 16)
            sp.dma_start(w2s[:, :, :], w2).then_inc(w2_in, 16)
            sp.dma_start(w3s[:, :], w3).then_inc(tail_in, 16)
            sp.dma_start(b2s[:, :], b2).then_inc(tail_in, 16)
            sp.wait_ge(y_ready, 1)
            sp.dma_start(out, y[:, :]).then_inc(y_out, 16)
            sp.wait_ge(y_out, 16)

        @block.gpsimd
        def _(pool):
            nc.gpsimd.memset(idle[:, :], 0.0).then_inc(idle_ready, 1)
            nc.gpsimd.memset(warm[:, 0:1], 0.0).then_inc(warm_zeroed, 1)
            nc.gpsimd.memset(cut[:, :, :], 0.0).then_inc(lanes_zeroed, 1)
            nc.gpsimd.memset(sums_e[:, :, :], 0.0).then_inc(sums_zeroed, 1)
            pool.wait_ge(ids_rows_in, 16)

            def gather(rows, n, c, done):
                at = c * NF + NS + n
                pool.indirect_dma_start(
                    out=rows, out_offset=None, in_=big[n][:, :],
                    in_offset=bass.IndirectOffsetOnAxis(ap=idr[:, at:at + 1], axis=0)).then_inc(done, 16)

            for n in range(EARLY):
                for c in range(NC):
                    gather(row_e[:, n, c, :], n, c, early_in[n])
            for c in range(NC):
                for n in range(LATE):
                    gather(row_l[:, c, n, :], EARLY + n, c, late_in[c])

        @block.scalar
        def _(act):
            act.dma_start(consts[:, :], digit_consts).then_inc(consts_in, 16)
            act.wait_ge(warm_zeroed, 1)
            nc.scalar.activation(warm[:, 1:2], warm[:, 0:1], ACT.Relu)
            act.wait_ge(kinds_zeroed, 1)
            act.wait_ge(consts_in, 16)

            def octet_kinds(o):
                rows = slice(P // NO * o, P // NO * (o + 1))
                nc.scalar.activation(kinds[rows, o, :], digit[rows, 0, :], ACT.Square,
                                     bias=step[rows, 0:1]).then_inc(kinds_ready, 1)

            def onehots(number, count):
                act.wait_ge(arg_ready, number + count)
                bank = number % BANKS
                nc.scalar.activation(onehot[:, number:number + count, :], acc[:, bank:bank + count, :],
                                     ACT.Relu).then_inc(onehot_ready, 1)

            act.wait_ge(digits_ready, 1)
            octet_kinds(0)
            act.wait_ge(digits_ready, 2)
            nc.scalar.activation(block_kinds[:, :], digit[:, 1, :], ACT.Square,
                                 bias=step[:, 1:2]).then_inc(block_kinds_ready, 1)
            for number in range(PAIR, NS + NG, PAIR):
                onehots(number, min(PAIR, NS + NG - number))
                if number in KINDS_AFTER:
                    octet_kinds(KINDS_AFTER.index(number) + 1)

            for s in range(len(STAGES)):
                act.wait_ge(turned, s + 1)
                nc.scalar.activation(sums_t[:, :], st[0:ROWS_T, :], ACT.Copy).then_inc(sums_t_ready, 1)
                act.wait_ge(factors, s + 1)
                if s >= 2:
                    act.wait_ge(z_ready, s - 1)
                nc.scalar.activation(first[:, s % 2, :], fa[:, :], ACT.Copy).then_inc(first_ready, 1)
            act.wait_ge(tail_in, 32)

            def samples(h):
                return slice(h * HALF, (h + 1) * HALF)

            def sums_t_late(h):
                act.wait_ge(turned, len(STAGES) + h + 1)
                nc.scalar.activation(sums_lt[:, samples(h)], late_t[:, samples(h)], ACT.Copy).then_inc(sums_t_ready, 1)

            def first_late(h):
                k = KE + h
                act.wait_ge(factors, k + 1)
                act.wait_ge(z_ready, k - 1)
                nc.scalar.activation(first[0:NL, k % 2, 0:HALF], fa[0:NL, 0:HALF], ACT.Copy).then_inc(first_ready, 1)

            def relu1(h, n):
                act.wait_ge(layer1, h * N1 + n + 1)
                nc.scalar.activation(h1[:, n, samples(h)], acc[:, n, samples(h)], ACT.Relu).then_inc(h1_ready, 1)

            def relu2(h):
                act.wait_ge(layer2[1], h + 1)
                nc.scalar.activation(h2[:, 1, samples(h)], st[:, 0:HALF], ACT.Relu,
                                     bias=b2s[:, 1:2]).then_inc(h2_ready[1], 1)

            sums_t_late(0)
            first_late(0)
            for n in range(N1):
                relu1(0, n)
            sums_t_late(1)
            first_late(1)
            relu2(0)
            for n in range(N1):
                relu1(1, n)
            relu2(1)

        @block.vector
        def _(dve):
            steps = [0]

            def mark(ins):
                steps[0] += 1
                ins.then_inc(dve_step, 1)
                return steps[0]

            def after(step):
                dve.wait_ge(dve_step, step)

            nc.vector.memset(kinds[:, :, :].bitcast(fp32), 0.0).then_inc(kinds_zeroed, 1)
            dve.wait_ge(ids_kinds_in, 16)
            dve.wait_ge(consts_in, 16)
            for n in range(2):
                nc.vector.tensor_scalar(digit[:, n, :], idk[:, :], consts[:, n:n + 1], None,
                                        ALU.bitwise_and).then_inc(digits_ready, 1)
            dve.wait_ge(arg_ready, PAIR)
            nc.vector.tensor_scalar(onehot[:, 0:PAIR, :], acc[:, 0:PAIR, :], 0.0, None,
                                    ALU.max).then_inc(first_pair_ready, 1)
            dve.wait_ge(lanes_zeroed, 1)

            def row_sums(g, n):
                a, b = halves[g][n]
                dve.wait_ge(table_in[2 * g + n], 16)
                return mark(nc.vector.tensor_reduce(
                    cut_of(a, b, 0), tab[:, BLOCK_AT[a]:BLOCK_AT[b], :].rearrange("p (t j) x -> p t j x", j=BLOCKS[a]),
                    axis=AX.X, op=ALU.add))

            def cut_rows(g, part):
                a, b = GROUPS[g]
                return nc.vector.tensor_tensor(cut_of(a, b, part), cut_of(a, b, part - 1),
                                               upper(cut_of(a, b, part - 1)), ALU.subtract)

            def keep_block(g):
                lanes_of = slice(0, LANE * (GROUPS[g][1] - GROUPS[g][0]))
                dve.wait_ge(picked, g + 1)
                wait_onehot(dve, mask_number(g))
                if g >= 2:
                    dve.wait_ge(summed, g - 1)
                nc.vector.tensor_tensor(kept[lanes_of, g % 2, :], pk[lanes_of, :], onehot[lanes_of, mask_number(g), :],
                                        ALU.mult).then_inc(kept_ready, 1)

            def sums_e_of(n, part):
                return sums_e[:, :, part * EARLY + n:(part + 1) * EARLY]

            def big_sums(n):
                dve.wait_ge(early_in[n], 16 * NC)
                return mark(nc.vector.tensor_reduce(sums_e_of(n, 0)[:, :, 0:1], row_e[:, n, :, :], axis=AX.X, op=ALU.add))

            def cut_big(n, part):
                return nc.vector.tensor_tensor(sums_e_of(n, part), sums_e_of(n, part - 1),
                                               upper(sums_e_of(n, part - 1)), ALU.subtract)

            def products(k):
                dve.wait_ge(first_ready, k + 1)
                nc.vector.tensor_tensor(z[:, k, :], first[:, k % 2, :], fb[:, :], ALU.mult).then_inc(z_ready, 1)

            for g in range(NG + 1):
                s = g - FIRST_STAGE
                new = g - 1 if s else 0
                if g < NG:
                    row_sums(g, 0)
                if g >= 1:
                    keep_block(g - 1)
                if g == NG:
                    break
                rows_done = row_sums(g, 1)
                if g == 1:
                    dve.wait_ge(sums_zeroed, 1)
                if s >= 1:
                    dve.wait_ge(turned, s)
                if g >= 1:
                    big_done = big_sums(g - 1)
                after(rows_done)
                rows_done = mark(cut_rows(g, 1))
                if s >= 0:
                    after(big_done)
                    big_done = mark(cut_big(new, 1))
                after(rows_done)
                cut_rows(g, 2).then_inc(cut_ready, 1)
                if s >= 0:
                    after(big_done)
                    cut_big(new, 2).then_inc(big_ready, 1)
                if 1 <= s < KE - 2:
                    products(s - 1)
            products(KE - 3)
            dve.wait_ge(turned, KE - 1)
            for n in range(NG - 1, EARLY):
                big_done = big_sums(n)
            after(big_done)
            after(mark(cut_big(NG - 1, 1)))
            cut_big(NG - 1, 2).then_inc(big_ready, 1)
            products(KE - 2)

            def samples(h):
                return slice(h * HALF, (h + 1) * HALF)

            def late_sums(h):
                chunks = slice(h * NC // NH, (h + 1) * NC // NH)
                for c in range(NC)[chunks]:
                    dve.wait_ge(late_in[c], 16 * LATE)
                after(mark(nc.vector.tensor_reduce(sums_l[:, chunks, 0, :], row_l[:, chunks, :, :], axis=AX.X, op=ALU.add)))
                after(mark(nc.vector.tensor_tensor(sums_l[:, chunks, 1, :], sums_l[:, chunks, 0, :],
                                                   upper(sums_l[:, chunks, 0, :]), ALU.subtract)))
                nc.vector.tensor_tensor(sums_l[:, chunks, 2, :], sums_l[:, chunks, 1, :],
                                        upper(sums_l[:, chunks, 1, :]), ALU.subtract).then_inc(big_ready, 1)

            def late_products(h):
                dve.wait_ge(first_ready, KE + h + 1)
                nc.vector.tensor_tensor(z[0:NL, KE, samples(h)], first[0:NL, (KE + h) % 2, 0:HALF],
                                        fb[0:NL, 0:HALF], ALU.mult).then_inc(z_ready, 1)

            def relu2(h):
                dve.wait_ge(layer2[0], h + 1)
                nc.vector.tensor_scalar(h2[:, 0, samples(h)], pk[:, 0:HALF], b2s[:, 0:1], 0.0,
                                        ALU.add, ALU.max).then_inc(h2_ready[0], 1)

            late_sums(0)
            products(KE - 1)
            late_products(0)
            late_sums(1)
            dve.wait_ge(tail_in, 32)
            relu2(0)
            late_products(1)
            relu2(1)
            dve.wait_ge(layer3_done, 1)
            nc.vector.tensor_copy(y[:, :], fa[:, 0:NC]).then_inc(y_ready, 1)

        @block.tensor
        def _(pe):
            def argument(number):
                g = next(g for g in range(NG) if number <= mask_number(g))
                if number >= BANKS:
                    wait_onehot(pe, number - BANKS)
                if number == mask_number(g):
                    pe.wait_ge(bcoef_in, 16)
                    pe.wait_ge(block_kinds_ready, 1)
                    coefs, squares = bcoef[:, g, :], block_kinds[:, :]
                else:
                    t = number - g
                    pe.wait_ge(kinds_ready, t // OCT + 1)
                    coefs, squares = coef[:, t % OCT, :], kinds[:, t // OCT, :]
                nc.tensor.matmul(acc[:, number % BANKS, :], coefs, squares, start=True, stop=True).then_inc(arg_ready, 1)

            def keep_warm(n):
                for _ in range(n):
                    nc.tensor.matmul(pk[:, :], idle[:, 0:P], idle[:, :], start=True, stop=True)

            def pick_rows(g):
                a, b = GROUPS[g]
                pe.wait_ge(cut_ready, g + 1)
                if g == 0:
                    wait_onehot(pe, 0)
                wait_onehot(pe, hot_number(g, b - 1))
                if g >= 1:
                    pe.wait_ge(kept_ready, g)
                for t in range(a, b):
                    last = nc.tensor.matmul(pk[LANE * (t - a):LANE * (t - a + 1), :], upper(cut[:, t, :]),
                                            onehot[:, hot_number(g, t), :], start=True, stop=True)
                last.then_inc(picked, 1)

            def add_blocks(g):
                a, b = GROUPS[g]
                rows = LANE * (b - a)
                pe.wait_ge(kept_ready, g + 1)
                if g > FIRST_STAGE:
                    pe.wait_ge(sums_t_ready, g - FIRST_STAGE)
                shift = NS - b
                nc.tensor.matmul(st[0:ROWS_T, :], lane_sum[0:rows, shift:shift + ROWS_T], kept[0:rows, g % 2, :],
                                 start=(g == 0), stop=False, skip_group_check=True).then_inc(summed, 1)

            def turn_sums(s):
                pe.wait_ge(big_ready, s + 1)
                if s >= 1:
                    pe.wait_ge(sums_t_ready, s)
                for c in range(NC):
                    last = nc.tensor.matmul(st[0:LANE, c * P:(c + 1) * P], upper(sums_e[:, c, :]), idn[:, :],
                                            start=True, stop=True, skip_group_check=True)
                last.then_inc(turned, 1)

            def early_factors(k):
                pe.wait_ge(sums_t_ready, k + 1)
                if k >= 1:
                    pe.wait_ge(z_ready, k)
                for side, bank in ((0, fa), (1, fb)):
                    last = nc.tensor.matmul(bank[:, :], picks[:, k, side, :], sums_t[:, :],
                                            start=True, stop=True)
                last.then_inc(factors, 1)

            def layer1_early(k, ns=range(N1)):
                pe.wait_ge(w1_in[k], 16)
                pe.wait_ge(z_ready, k + 1)
                for n in ns:
                    nc.tensor.matmul(acc[:, n, :], w1s[:, k, n * P:(n + 1) * P], z[:, k, :],
                                     start=(k == 0), stop=False, skip_group_check=True)

            def turn_late(h):
                pe.wait_ge(big_ready, len(STAGES) + h + 1)
                pe.wait_ge(z_ready, KE + h)
                for c in range(h * NC // NH, (h + 1) * NC // NH):
                    last = nc.tensor.transpose(late_t[:, c * P:(c + 1) * P],
                                               upper(sums_l[:, c, :, :].rearrange("p k f -> p (k f)")), idn[:, :])
                last.then_inc(turned, 1)

            def samples(h):
                return slice(h * HALF, (h + 1) * HALF)

            def late_factors(h):
                pe.wait_ge(sums_t_ready, len(STAGES) + h + 1)
                nc.tensor.matmul(fa[0:NL, 0:HALF], picks[:, KE, 0, 0:NL], sums_t[:, samples(h)],
                                 start=True, stop=False)
                nc.tensor.matmul(fa[0:NL, 0:HALF], picks_l[:, 0, :], sums_lt[:, samples(h)], start=False, stop=True)
                nc.tensor.matmul(fb[0:NL, 0:HALF], picks_l[:, 1, :], sums_lt[:, samples(h)],
                                 start=True, stop=True).then_inc(factors, 1)

            def layer1_late(h):
                pe.wait_ge(z_ready, KE + h + 1)
                for n in range(N1):
                    if h >= 1:
                        pe.wait_ge(h1_ready, (h - 1) * N1 + n + 1)
                    nc.tensor.matmul(acc[:, n, samples(h)], w1s[:, KE, n * P:(n + 1) * P], z[:, KE, samples(h)],
                                     start=False, stop=True, skip_group_check=True).then_inc(layer1, 1)

            def layer2_half(h, m, ns=range(N1)):
                if h >= 1 and ns[0] == 0:
                    pe.wait_ge(h2_ready[m], h)
                for n in ns:
                    if m == 0:
                        pe.wait_ge(h1_ready, h * N1 + n + 1)
                    last = nc.tensor.matmul(l2[m][:, 0:HALF], w2s[:, n, m * P:(m + 1) * P], h1[:, n, samples(h)],
                                            start=(n == 0), stop=(n == N1 - 1))
                if ns[-1] == N1 - 1:
                    last.then_inc(layer2[m], 1)

            def layer3(m, c):
                pe.wait_ge(h2_ready[m], c * NH // NC + 1)
                return nc.tensor.matmul(fa[:, c:c + 1], h2[:, m, c * P:(c + 1) * P], w3s[:, m:m + 1],
                                        start=(m == 0 and c == 0), stop=(m == N2 - 1), skip_group_check=True)

            pe.wait_ge(coef_in, 16)
            for number in range(AHEAD[0]):
                argument(number)
            pick_rows(0)
            for g in range(1, NG + 1):
                if g < len(AHEAD):
                    for number in range(AHEAD[g - 1], AHEAD[g]):
                        argument(number)
                k = g - 1 - FIRST_STAGE
                if g == 1:
                    pe.wait_ge(lanes_in, 16)
                add_blocks(g - 1)
                if k == 0:
                    pe.wait_ge(idle_ready, 1)
                    pe.wait_ge(ident_in, 16)
                    pe.wait_ge(picks_in, 32)
                if k == KE - 2:
                    pe.wait_ge(picks_rest_in, 16)
                if k >= 0:
                    turn_sums(k)
                if k == 0:
                    keep_warm(4)
                if k >= 1:
                    layer1_early(k - 1, range(2, 3) if g < NG else range(1))
                if k >= 0:
                    early_factors(k)
                if k == 0:
                    keep_warm(4)
                if g < NG:
                    pick_rows(g)
                if k >= 1:
                    layer1_early(k - 1, range(3, N1) if g < NG else range(1, N1))
                if k == 0:
                    wait_onehot(pe, NS + NG - 1)
                if k >= 0 and g < NG - 1:
                    layer1_early(k, range(2))
            layer1_early(KE - 2, range(1))
            turn_sums(KE - 1)
            layer1_early(KE - 2, range(1, 2))
            early_factors(KE - 1)
            layer1_early(KE - 2, range(2, N1))
            layer1_early(KE - 1, range(1))
            turn_late(0)
            layer1_early(KE - 1, range(1, 2))
            late_factors(0)
            layer1_early(KE - 1, range(2, N1))
            pe.wait_ge(w1_in[KE], 16)
            pe.wait_ge(dense_in, 16)
            layer1_late(0)
            pe.wait_ge(w2_in, 16)
            layer2_half(0, 0, range(N1 // 2))
            turn_late(1)
            layer2_half(0, 0, range(N1 // 2, N1))
            late_factors(1)
            layer2_half(0, 1)
            layer1_late(1)
            pe.wait_ge(tail_in, 32)
            layer2_half(1, 0)
            layer3(0, 0)
            layer3(0, 1)
            layer2_half(1, 1)
            for m, c in ((1, 0), (1, 1), (0, 2), (0, 3), (1, 2), (1, 3)):
                last = layer3(m, c)
            last.then_inc(layer3_done, 1)


def kernel(**inputs):
    import ml_dtypes
    import numpy as np
    import concourse.bacc as bacc
    from concourse.bass_utils import run_bass_kernel_spmd

    a = {k: np.asarray(v) for k, v in inputs.items()}
    ids = a["ids"]
    arrays = {}
    arrays["ids_rows"] = np.ascontiguousarray(
        ids[:, SMALL + BIG].reshape(NC, P, NF).transpose(1, 0, 2).reshape(P, NC * NF))
    slots = np.zeros((NO, SLOTS, BATCH), ids.dtype)
    slots[:, :OCT] = ids[:, SMALL].T.reshape(NO, OCT, BATCH)
    arrays["ids_kinds"] = np.repeat(slots[:, None], KINDS, axis=1).reshape(P, BATCH)
    tables = np.zeros((P, BLOCK_AT[NS], EMB), np.float32)
    for t, f in enumerate(SMALL):
        padded = np.zeros((BLOCKS[t] * P, EMB), np.float32)
        padded[:ROWS[f]] = a[f"tbl_{f}"]
        tables[:, BLOCK_AT[t]:BLOCK_AT[t + 1]] = padded.reshape(BLOCKS[t], P, EMB).transpose(1, 0, 2)
    arrays["tables"] = tables
    for n, f in enumerate(BIG):
        arrays[f"big{n}"] = np.ascontiguousarray(a[f"tbl_{f}"])
    kind = np.tile(np.repeat(np.arange(KINDS), SLOTS), NO)
    field = np.repeat(np.arange(NO), KINDS * SLOTS) * OCT + np.tile(np.arange(SLOTS), NO * KINDS)
    field[np.arange(P) % SLOTS == OCT] = -1
    plus = np.stack([kind % 2 * np.where(kind < 2, HIGH_1, LOW_1), kind % 2 * BLOCK_1], axis=1).astype(np.float32)
    arrays["digit_consts"] = np.concatenate(
        [np.stack([np.where(kind < 2, HIGH, LOW), np.full(P, BLOCK)], axis=1).astype(np.int32), plus.view(np.int32)], axis=1)
    p = np.arange(P)
    high, low = p // HIGH_1, p % HIGH_1
    blk = p % LANE % MAXB
    coef = np.zeros((KINDS, SLOTS, OCT, P), ml_dtypes.bfloat16)
    for i in range(OCT):
        coef[0, i, i], coef[1, i, i], coef[1, OCT, i] = np.stack([-1 - high, high, -high * (high + 1)]) / HIGH_1 ** 2
        coef[2, i, i], coef[3, i, i], coef[3, OCT, i] = -1 - low, low, 1 - low * (low + 1)
    arrays["digit_coef"] = np.tile(coef.reshape(KINDS * SLOTS, OCT, P), (NO, 1, 1))
    block_coef = np.zeros((P, NG, P), ml_dtypes.bfloat16)
    block_coef[SLOTS + OCT] = (1 - blk * (blk + 1)) / BLOCK_1 ** 2
    lanes = np.zeros((P, ROWS_T + NS - P // LANE), ml_dtypes.bfloat16)
    for g, (t0, t1) in enumerate(GROUPS):
        for t in range(t0, t1):
            lane = slice(LANE * (t - t0), LANE * (t - t0 + 1))
            block_coef[(field == t) & (kind == 0), g, lane] = (-1 - blk[lane]) / BLOCK_1 ** 2
            block_coef[(field == t) & (kind == 1), g, lane] = blk[lane] / BLOCK_1 ** 2
    for t in range(P // LANE):
        for part in range(3):
            at = t * LANE + part * MAXB
            lanes[at:at + MAXB, LANE + part * NS + GROUPS[-1][0] + t] = 1
    arrays["block_coef"] = block_coef
    arrays["lanes"] = lanes
    row_of = {f: LANE + t + NS * np.arange(3) for t, f in enumerate(SMALL)}
    row_of |= {f: n + EARLY * np.arange(3) for n, f in enumerate(BIG[:EARLY])}
    row_of |= {f: ROWS_T + n + LATE * np.arange(3) for n, f in enumerate(BIG[EARLY:])}
    pick = np.zeros((ROWS_T + 3 * LATE, KC, 2, P), ml_dtypes.bfloat16)
    for at, pairs in ((0, EARLY_PAIRS), (KE * P, LATE_PAIRS)):
        for n, pair in enumerate(pairs, at):
            for side in range(2):
                pick[row_of[ORDER[pair[side]]], n // P, side, n % P] = 1
    arrays["pick"] = pick[:ROWS_T]
    arrays["pick_late"] = np.ascontiguousarray(pick[ROWS_T:, KE, :, :NL])
    arrays["ident"] = np.eye(P, dtype=ml_dtypes.bfloat16)
    arrays["dense_t"] = np.concatenate([a["dense_ctx"].T, np.ones((1, BATCH), np.float32)])
    row = {pair: n for n, pair in enumerate((i, j) for i in range(NF) for j in range(i + 1, NF))}

    def w_row(i, j):
        f, g = ORDER[i], ORDER[j]
        return row[min(f, g), max(f, g)]

    w1 = np.zeros((KC * P, H1), np.float32)
    w1[:len(EARLY_PAIRS)] = a["W_top1"][[w_row(*q) for q in EARLY_PAIRS]]
    w1[KE * P:KE * P + NL] = a["W_top1"][[w_row(*q) for q in LATE_PAIRS]]
    w1[KE * P + NL:KC * P - 1] = a["W_top1"][len(row):]
    w1[KC * P - 1] = a["b_top1"]
    arrays["w1"] = np.ascontiguousarray(w1.reshape(KC, P, H1).transpose(1, 0, 2))
    arrays["w2"] = np.ascontiguousarray(a["W_top2"].reshape(N1, P, H2).transpose(1, 0, 2))
    arrays["b2"] = np.ascontiguousarray(a["b_top2"].reshape(N2, P).T)
    arrays["w3"] = np.ascontiguousarray(a["W_top3"].reshape(N2, P).T)

    nc = bacc.Bacc("TRN2", target_bir_lowering=False, num_devices=1)
    aps = {k: nc.dram_tensor(f"in_{k}", v.shape, mybir.dt.from_np(v.dtype), kind="ExternalInput").ap()
           for k, v in arrays.items()}
    out = nc.dram_tensor("out_y", (P, NC), mybir.dt.float32, kind="ExternalOutput").ap()
    big = [aps.pop(f"big{n}") for n in range(NB)]
    build_tower(nc, big=big, out=out, **aps)
    r = run_bass_kernel_spmd(nc, [{f"in_{k}": v for k, v in arrays.items()}], core_ids=[0])
    return np.ascontiguousarray(r.results[0]["out_y"].T).reshape(BATCH, 1)
```
